# Optimizing a Trainium2 kernel written in Bass

```python
import numpy as np
import jax
import jax.numpy as jnp

def _softmax(x, axis=-1):
    return jax.nn.softmax(x, axis=axis)

def _gelu(x):
    return jax.nn.gelu(x, approximate=True)

def _silu(x):
    return jax.nn.silu(x)

def _sigmoid(x):
    return jax.nn.sigmoid(x)

def _layernorm(x, axis=-1, eps=1e-05):
    m = jnp.mean(x, axis=axis, keepdims=True)
    v = jnp.var(x, axis=axis, keepdims=True)
    return (x - m) / jnp.sqrt(v + eps)

def _scatter_add(tgt, idx, src, axis=0):
    return tgt.at[idx].add(src)

def _segment_sum(src, seg, n):
    return jax.ops.segment_sum(src, seg, n)
kernel_name = 'mk_macaron_d1_jaxref_r8_393d83'

def setup_inputs(seed: int=0):
    np.random.seed(seed)
    _w = jnp.asarray

    def _L0_attn_setup():
        import math
        import jax, jax.numpy as jnp
        import numpy as np
        BATCH, LENGTH, D_MODEL, D_STATE = (8, 256, 128, 64)
        DT_MIN, DT_MAX = (0.001, 0.1)
        key = jax.random.key(seed)
        k1, k2, k3, k4 = jax.random.split(key, 4)
        x = jax.random.normal(k1, (BATCH, LENGTH, D_MODEL), dtype=jnp.float32)
        log_dt = jax.random.uniform(k2, (D_MODEL,), dtype=jnp.float32) * (math.log(DT_MAX) - math.log(DT_MIN)) + math.log(DT_MIN)
        scale = 1.0 / math.sqrt(D_STATE)
        B = jax.random.normal(k3, (D_MODEL, D_STATE), dtype=jnp.float32) * scale
        C = jax.random.normal(k4, (D_MODEL, D_STATE), dtype=jnp.float32) * scale
        D = jnp.ones((D_MODEL,), dtype=jnp.float32)
        return {'x': x, 'log_dt': log_dt, 'B': B, 'C': C, 'D': D}
    _L0_attn_in = _L0_attn_setup()

    def _L0_ffn_setup():
        import jax, jax.numpy as jnp
        import numpy as np
        N_EMBD = 128
        N_EXPERTS = 8
        TOP_K = 2
        B, T = (4, 256)
        key = jax.random.key(seed)
        ks = jax.random.split(key, 8)
        C, E, H = (N_EMBD, N_EXPERTS, 4 * N_EMBD)
        s_in = 1.0 / np.sqrt(C)
        s_hid = 1.0 / np.sqrt(H)
        x = jax.random.normal(ks[0], (B, T, C), dtype=jnp.float32)
        W1 = jax.random.uniform(ks[1], (E, C, H), minval=-s_in, maxval=s_in, dtype=jnp.float32)
        b1 = jax.random.uniform(ks[2], (E, H), minval=-s_in, maxval=s_in, dtype=jnp.float32)
        W2 = jax.random.uniform(ks[3], (E, H, C), minval=-s_hid, maxval=s_hid, dtype=jnp.float32)
        b2 = jax.random.uniform(ks[4], (E, C), minval=-s_hid, maxval=s_hid, dtype=jnp.float32)
        Wg = jax.random.uniform(ks[5], (C, E), minval=-s_in, maxval=s_in, dtype=jnp.float32)
        bg = jax.random.uniform(ks[6], (E,), minval=-s_in, maxval=s_in, dtype=jnp.float32)
        return {'x': x, 'W1': W1, 'b1': b1, 'W2': W2, 'b2': b2, 'Wg': Wg, 'bg': bg}
    _L0_ffn_in = _L0_ffn_setup()
    _d = {'L0_attn_x': _L0_attn_in['x'], 'L0_attn_log_dt': _L0_attn_in['log_dt'], 'L0_attn_B': _L0_attn_in['B'], 'L0_attn_C': _L0_attn_in['C'], 'L0_attn_D': _L0_attn_in['D'], 'L0_ffn_W1': _L0_ffn_in['W1'], 'L0_ffn_b1': _L0_ffn_in['b1'], 'L0_ffn_W2': _L0_ffn_in['W2'], 'L0_ffn_b2': _L0_ffn_in['b2'], 'L0_ffn_Wg': _L0_ffn_in['Wg'], 'L0_ffn_bg': _L0_ffn_in['bg']}
    _x0 = _d['L0_attn_x']
    _d['L0_attn_x'] = jax.random.normal(jax.random.fold_in(jax.random.key(seed), 1), (16, 256, 128), dtype=_x0.dtype)
    del _x0
    return _d

def reference(L0_attn_x, L0_attn_log_dt, L0_attn_B, L0_attn_C, L0_attn_D, L0_ffn_W1, L0_ffn_b1, L0_ffn_W2, L0_ffn_b2, L0_ffn_Wg, L0_ffn_bg):

    def _L0_attn_ref(x, log_dt, B, C, D):
        import math
        import jax, jax.numpy as jnp
        import numpy as np
        BATCH, LENGTH, D_MODEL, D_STATE = (8, 256, 128, 64)
        DT_MIN, DT_MAX = (0.001, 0.1)
        "S4DKernel.forward(x, mode='conv') -> y of shape [batch, length, d_model]."
        d_model, d_state = B.shape
        length = x.shape[1]
        A = -0.5 * jnp.arange(1, d_state + 1, dtype=jnp.float32)
        dt = jnp.exp(log_dt)
        dtA = dt[:, None] * A[None, :]
        A_bar = jnp.exp(dtA)
        B_bar = jnp.expm1(dtA) / A[None, :] * B
        k_range = jnp.arange(length, dtype=jnp.float32)
        log_A_bar = jnp.log(jnp.clip(A_bar, 1e-10))
        powers = jnp.exp(log_A_bar[:, :, None] * k_range[None, None, :])
        kernel = jnp.einsum('dn,dnk->dk', C * B_bar, powers)
        x_t = jnp.swapaxes(x, 1, 2)
        fft_size = 2 * length
        x_f = jnp.fft.rfft(x_t, n=fft_size)
        k_f = jnp.fft.rfft(kernel, n=fft_size)
        y = jnp.fft.irfft(x_f * k_f[None], n=fft_size)[..., :length]
        y = y + D[None, :, None] * x_t
        return jnp.swapaxes(y, 1, 2)

    def _L0_ffn_ref(x, W1, b1, W2, b2, Wg, bg):
        import jax, jax.numpy as jnp
        import numpy as np
        N_EMBD = 128
        N_EXPERTS = 8
        TOP_K = 2
        B, T = (4, 256)
        gate_scores = jax.nn.softmax(jnp.einsum('btc,ce->bte', x, Wg) + bg, axis=-1)
        h = jax.nn.relu(jnp.einsum('btc,ech->bteh', x, W1) + b1)
        expert_out = jnp.einsum('bteh,ehc->btec', h, W2) + b2
        topk_scores, topk_idx = jax.lax.top_k(gate_scores, TOP_K)
        top_probs = jax.nn.softmax(topk_scores, axis=-1)
        sel = jnp.take_along_axis(expert_out, topk_idx[..., None], axis=2)
        out = jnp.sum(sel * top_probs[..., None], axis=2)
        return out
    x = L0_attn_x
    x = x + 0.5 * _L0_ffn_ref(_layernorm(x, axis=-1), L0_ffn_W1, L0_ffn_b1, L0_ffn_W2, L0_ffn_b2, L0_ffn_Wg, L0_ffn_bg)
    x = x + _L0_attn_ref(_layernorm(x, axis=-1), L0_attn_log_dt, L0_attn_B, L0_attn_C, L0_attn_D)
    x = x + 0.5 * _L0_ffn_ref(_layernorm(x, axis=-1), L0_ffn_W1, L0_ffn_b1, L0_ffn_W2, L0_ffn_b2, L0_ffn_Wg, L0_ffn_bg)
    return x

_drawn_inputs = setup_inputs


def setup_inputs(seed=0):
    import zlib

    import numpy as np

    out = dict(_drawn_inputs(seed))
    spreads = {'L0_attn_D': (1.0, 0.2)}
    factors = {'L0_attn_log_dt': 64.0,
     'L0_attn_B': 64.0,
     'L0_attn_C': 64.0,
     'L0_ffn_b1': 5.063,
     'L0_ffn_b2': 4.234}
    for name, (base, spread) in spreads.items():
        noise = np.random.default_rng([zlib.crc32(name.encode()), seed]).standard_normal(out[name].shape)
        drawn = base * np.exp(spread * noise) if base else spread * noise
        out[name] = jnp.asarray(drawn.astype(out[name].dtype))
    for name, factor in factors.items():
        out[name] = (out[name] * factor).astype(out[name].dtype)
    return out
```

```python
import concourse.bass as bass
from concourse import mybir
from contextlib import ExitStack

P = 128
BATCH, LENGTH, D = 16, 256, 128
N_STATE = 64
E, HID, TOP_K = 8, 512, 2
HC = HID // P
NT = BATCH * LENGTH // P
G = 2
TG = NT // G
ST = (TG * P * TOP_K - E) // P + E
LAYERS = 2
EPS = 1e-5
LOG_FLOOR = -23.025850929940457
XS_RING, YS_RING, XN_RING, YG_RING = 4, 4, 4, 3
SC_SEMS = 8
EXPONENT = 0x7F800000
KPAD = LENGTH + P
CB = 32
TC = 16
T_PARTS = D // TC
T_PLACES = T_PARTS - 1


def toeplitz_place(part, g):
    return part if part not in (0, T_PARTS - 1) else (0 if part else (0 if g == 0 else 2))


def conv_blocks(g):
    return [0, 1, 2, 3] if g == 0 else [1, 2, 3, 0]


def run_steps(eng, first, last, unroll, peel, step):
    n = first
    while n < last and (n < peel or n % unroll):
        step(n, n % unroll)
        n += 1
    rounds = (last - n) // unroll
    if rounds > 1:
        with eng.Fori(0, rounds) as r:
            for u in range(unroll):
                step(r * unroll + (n + u), u)
        n += rounds * unroll
    while n < last:
        step(n, n % unroll)
        n += 1


def macaron_kernel(nc, x, log_dt, s4_b, s4_c, s4_d, w1, b1, w2, b2, wg, bg, out):
    F32, F16, I32, U32 = mybir.dt.float32, mybir.dt.float16, mybir.dt.int32, mybir.dt.uint32
    ALU, ACT, AX = mybir.AluOpType, mybir.ActivationFunctionType, mybir.AxisListType
    RMAX = bass.bass_isa.ReduceOp.max

    with ExitStack() as ctx:
        def sb(name, shape, dt=F32):
            return ctx.enter_context(nc.sbuf_tensor(name, shape, dt))

        def sem(name):
            return ctx.enter_context(nc.semaphore(name))

        def sems(name, n):
            return [sem(f"{name}{i}") for i in range(n)]

        slot_x = [nc.dram_tensor(f"slot_x{g}", [ST * P, 2 * D], F16, kind="Internal").ap() for g in range(G)]
        slot_y = [[nc.dram_tensor(f"slot_y{l}{g}", [ST * P, D], F32, kind="Internal").ap()
                   for g in range(G)] for l in range(LAYERS)]
        kern_d = nc.dram_tensor("kern_d", [P, 2 * KPAD], F16, kind="Internal").ap()

        xa = sb("xa", [P, NT, D])
        xhl = sb("xhl", [P, NT, 2, D], F16)
        w1hl = sb("w1hl", [P, E * 2 * HC * P], F16)
        w2hl = sb("w2hl", [P, E * 2 * HC * D], F16)
        toep = sb("toep", [P, T_PLACES * TC, 2 * LENGTH], F16)
        b2rep = sb("b2rep", [P, E * D])
        b1s = sb("b1s", [P, E * HC])
        wgs = sb("wgs", [P, E])
        bgs = sb("bgs", [P, E])
        ds4 = sb("ds4", [P, D])
        ident = sb("ident", [P, P])
        ident16 = sb("ident16", [P, P], F16)
        before16 = sb("before16", [P, P], F16)
        ones16 = sb("ones16", [P, P], F16)
        back16 = sb("back16", [P, P], F16)
        kinv = sb("kinv", [P, D])
        wsc = sb("wsc", [P, 8])
        wmax = sb("wmax", [P, 2])
        xs = sb("xs", [P, XS_RING, 2 * D], F16)
        xt = sb("xt", [P, 2, 2 * P], F16)
        hr = sb("hr", [P, 2, HID])
        hh = sb("hh", [P, 2, HID], F16)
        hl = sb("hl", [P, 2, HID], F16)
        ysb = sb("ysb", [P, YS_RING, D])
        yg = sb("yg", [P, YG_RING, TOP_K, D])
        xn = sb("xn", [P, XN_RING, D])
        xnt = hl[:, :, :].rearrange("p a b -> p (a b)").bitcast(F32).rearrange("p (a b) -> p a b", a=4)
        TE = TG * E
        mv = sb("mv", [P, TG, 2])
        spare = hr[:, :, :].rearrange("p a b -> p (a b)")
        st6 = spare[:, 0:TG * 6].rearrange("p (t s) -> p t s", s=6)
        rstd = sb("rstd", [P, TG])
        lg = sb("lg", [P, TG, E])
        sc = sb("sc", [P, TG, E])
        eq = sb("eq", [P, TG, E])
        oh = [sb(f"oh{k}", [P, TG, E], F16) for k in range(TOP_K)]
        ohs = sb("ohs", [P, TG, E], F16)
        m1 = sb("m1", [P, TG])
        m2 = sb("m2", [P, TG])
        mt = sb("mt", [P, TG])
        nv, nt1 = m1, mt
        tot = sb("tot", [P, E, TG])
        cum = sb("cum", [P, E, TG])
        pos = sb("pos", [P, TG, E])
        cnt = sb("cnt", [P, E])
        cnti = sb("cnti", [P, E], I32)
        ends = sb("ends", [P, E])
        slotf = sb("slotf", [P, TG])
        slots = sb("slots", [P, LAYERS * G, TOP_K, TG], I32)
        prob = sb("prob", [P, LAYERS * G, TOP_K, TG])
        et1 = xn[:, :, :].rearrange("p a b -> p (a b)")[0:1, 0:ST * E].rearrange("p (j e) -> p j e", e=E)
        et2 = sb("et2", [1, ST])
        etab = sb("etab", [1, LAYERS * G * ST], I32)
        prio = sb("prio", [P, E])
        segm = sb("segm", [P, E, TG], F16)
        one8 = sb("one8", [P, E])
        tstart = sb("tstart", [1, ST, E], F16)
        zero16 = xt[:, 0, :]
        tview = toep[:, :, :].rearrange("p a b -> p (a b)").bitcast(F32)
        used = [0]

        def scratch(n):
            used[0] += n
            assert used[0] <= T_PLACES * TC * LENGTH
            return tview[:, used[0] - n:used[0]]

        w1st, w2st = scratch(E * HID), scratch(E * HID)
        kramp = scratch(LENGTH)
        kexp = [scratch(LENGTH) for _ in range(4)]
        kacc = scratch(LENGTH)
        kpad = scratch(KPAD).bitcast(F16).rearrange("p (k s) -> p k s", s=2)
        nar, dta, loga, th, rden, rn, kw, sbt, sct = (scratch(N_STATE) for _ in range(9))
        ldt, dtt, kmx, kal, kiv = (scratch(1) for _ in range(5))
        kdiag = scratch(P)
        onesf = scratch(P)

        bank = [ctx.enter_context(nc.psum_tensor(f"bank{i}", [P, 512], F32)) for i in range(8)]
        HB, XB, YB, CBK = bank[0:2], bank[2:4], bank[4:6], bank[6:8]
        LG = XB[0]

        s_x = sems("s_x", 4)
        s_w1, s_w2, s_b1, s_b2, s_wg, s_s4, s_d = (sem(n) for n in ("s_w1", "s_w2", "s_b1", "s_b2", "s_wg", "s_s4", "s_d"))
        s_zero = sem("s_zero")
        s_zfill = sem("s_zfill")
        s_const = sem("s_const")
        s_id = sem("s_id")
        s_chain = sem("s_chain")
        s_ac = sem("s_ac")
        s_wmax = sem("s_wmax")
        s_wall = sem("s_wall")
        s_wh = sem("s_wh")
        s_wready = sem("s_wready")
        s_kin = sem("s_kin")
        s_kt = sem("s_kt")
        s_kexp = sem("s_kexp")
        s_kacc = sem("s_kacc")
        s_kpad = sem("s_kpad")
        s_kst = sem("s_kst")
        s_kdiag = sem("s_kdiag")
        s_kinv = sem("s_kinv")
        s_kinvc = sem("s_kinvc")
        s_toep = sems("s_toep", T_PARTS)
        s_tagain = sem("s_tagain")
        s_xn = sem("s_xn")
        s_xl = sem("s_xl")
        s_xnt = sem("s_xnt")
        s_xntc = sem("s_xntc")
        s_gate = sem("s_gate")
        s_logit = sem("s_logit")
        s_rsub = sem("s_rsub")
        s_rexp = sem("s_rexp")
        s_oh = sem("s_oh")
        s_pre = sem("s_pre")
        s_route = sem("s_route")
        s_scat = sems("s_scat", SC_SEMS)
        s_xs = sems("s_xs", XS_RING)
        s_xt = sem("s_xt")
        s_xtc = sem("s_xtc")
        s_h = sem("s_h")
        s_relu = sem("s_relu")
        s_hh = sem("s_hh")
        s_hl = sem("s_hl")
        s_y = sem("s_y")
        s_yc = sem("s_yc")
        s_yst = sems("s_yst", YS_RING)
        s_yg = [sems(f"s_yg{k}", YG_RING) for k in range(TOP_K)]
        s_comb = sem("s_comb")
        s_rev = sem("s_rev")
        s_revc = sem("s_revc")
        s_cv = sem("s_cv")
        s_cve = sem("s_cve")
        s_out = sem("s_out")

        x_t = x.rearrange("b (h p) c -> p (b h) c", p=P)
        out_t = out.rearrange("b (h p) c -> p (b h) c", p=P)
        lg_of = lambda layer, g: layer * G + g

        block = ctx.enter_context(nc.Block())

        @block.sync
        def _(sp):
            XQ = NT // 4
            sp.dma_start(xa[:, 0:XQ, :], x_t[:, 0:XQ, :]).then_inc(s_x[0], 16)
            sp.dma_start(xa[:, XQ:2 * XQ, :], x_t[:, XQ:2 * XQ, :]).then_inc(s_x[1], 16)
            sp.dma_start(wgs[:, :], wg).then_inc(s_wg, 16)
            sp.dma_start(bgs[:, :], bg.rearrange("(a e) -> a e", a=1).to_broadcast([P, E])).then_inc(s_wg, 16)
            sp.dma_start(w1st.rearrange("p (e h) -> p e h", e=E), w1.rearrange("e c h -> c e h")).then_inc(s_w1, 16)
            sp.dma_start(w2st.rearrange("p (e h) -> p e h", e=E),
                         w2.rearrange("e (p k) c -> p e (k c)", k=HC)).then_inc(s_w2, 16)
            sp.dma_start(xa[:, 2 * XQ:3 * XQ, :], x_t[:, 2 * XQ:3 * XQ, :]).then_inc(s_x[2], 16)
            sp.dma_start(xa[:, 3 * XQ:, :], x_t[:, 3 * XQ:, :]).then_inc(s_x[3], 16)
            sp.wait_ge(s_kpad, 1)
            sp.dma_start(kern_d, kpad.rearrange("p k s -> p (k s)")).then_inc(s_kst, 16)
            sp.wait_ge(s_kst, 16)
            sp.wait_ge(s_wready, 1)
            sp.wait_ge(s_kinvc, 1)

            def load_toeplitz(part, g, signal):
                src = bass.AP(kern_d.tensor, 2 + part * TC * 2 * KPAD, [[2, P], [2 * KPAD, TC], [1, 2 * LENGTH]])
                at = toeplitz_place(part, g) * TC
                sp.dma_start(toep[:, at:at + TC, :], src).then_inc(signal, 16)

            STORE_LAG = 6

            def expert_io(layer, g):
                base = lg_of(layer, g) * ST
                for k in range(SC_SEMS):
                    sp.wait_ge(s_scat[k], 16 * (lg_of(layer, g) + 1) * (TG * TOP_K // SC_SEMS))

                def load(n, u):
                    if not isinstance(n, int) or n >= XS_RING:
                        sp.wait_ge(s_xt, n - (XS_RING - 1))
                    row = (n - base) * P
                    sp.dma_start(xs[:, u, :], slot_x[g][bass.ds(row, P), :]).then_inc(s_xs[u], 16)

                def store(n, u):
                    sp.wait_ge(s_yc, n + 1)
                    sp.dma_start(slot_y[layer][g][bass.ds((n - base) * P, P), :], ysb[:, u, :]).then_inc(s_yst[u], 16)

                def step(n, u):
                    load(n, u)
                    if not isinstance(n, int) or n >= base + STORE_LAG:
                        store(n - STORE_LAG, (u - STORE_LAG) % 4)
                run_steps(sp, base, base + ST, 4, base + STORE_LAG, step)
                for n in range(base + ST - STORE_LAG, base + ST):
                    store(n, n % 4)

            for i in range(T_PLACES):
                load_toeplitz(i, 0, s_toep[i])
            for g in range(G):
                expert_io(0, g)
            sp.wait_ge(s_cv, 1)
            load_toeplitz(T_PARTS - 1, 0, s_toep[T_PARTS - 1])
            sp.wait_ge(s_cv, D // CB + 1)
            load_toeplitz(0, 1, s_tagain)
            for g in range(G):
                expert_io(1, g)
            for t in range(NT):
                sp.wait_ge(s_comb, NT + t + 1)
                sp.dma_start(out_t[:, t, :], xa[:, t, :]).then_inc(s_out, 16)
            sp.wait_ge(s_out, 16 * NT)

        @block.gpsimd
        def _(pool):
            done = [0]

            def link(ins):
                done[0] += 1
                ins.then_inc(s_id, 1)
                pool.wait_ge(s_id, done[0])

            nc.gpsimd.memset(zero16, 0.0).then_inc(s_zero, 1)
            link(nc.gpsimd.memset(ident[:, :], 0.0))
            nc.gpsimd.affine_select(out=ident[:, :], in_=ident[:, :], compare_op=ALU.not_equal, fill=1.0,
                                    base=0, pattern=[[-1, P]], channel_multiplier=1).then_inc(s_const, 1)
            link(nc.gpsimd.memset(ident16[:, :], 0.0))
            nc.gpsimd.affine_select(out=ident16[:, :], in_=ident16[:, :], compare_op=ALU.not_equal, fill=1.0,
                                    base=0, pattern=[[-1, P]], channel_multiplier=1).then_inc(s_const, 1)
            link(nc.gpsimd.memset(back16[:, :], 0.0))
            nc.gpsimd.affine_select(out=back16[:, :], in_=back16[:, :], compare_op=ALU.not_equal, fill=1.0,
                                    base=1 - P, pattern=[[1, P]], channel_multiplier=1).then_inc(s_const, 1)
            nc.gpsimd.memset(ones16[:, :], 1.0).then_inc(s_const, 1)
            nc.gpsimd.memset(onesf, 1.0).then_inc(s_const, 1)
            nc.gpsimd.memset(one8[:, :], 1.0).then_inc(s_const, 1)
            link(nc.gpsimd.memset(before16[:, :], 1.0))
            nc.gpsimd.affine_select(out=before16[:, :], in_=before16[:, :], compare_op=ALU.is_gt, fill=0.0,
                                    base=0, pattern=[[1, P]], channel_multiplier=-1).then_inc(s_const, 1)
            link(nc.gpsimd.memset(segm[:, :, :], 1.0))
            nc.gpsimd.memset(segm[:, :, 0:1], 0.0).then_inc(s_const, 1)
            nc.gpsimd.iota(prio[:, :], pattern=[[-1, E]], base=E, channel_multiplier=0,
                           allow_small_or_imprecise_dtypes=True).then_inc(s_const, 1)
            nc.gpsimd.iota(tstart[:, :, :], pattern=[[P, ST], [0, E]], base=0, channel_multiplier=0,
                           allow_small_or_imprecise_dtypes=True).then_inc(s_const, 1)
            nc.gpsimd.iota(nar, pattern=[[1, N_STATE]], base=1, channel_multiplier=0,
                           allow_small_or_imprecise_dtypes=True).then_inc(s_const, 1)
            nc.gpsimd.iota(kramp, pattern=[[1, LENGTH]], base=0, channel_multiplier=0,
                           allow_small_or_imprecise_dtypes=True).then_inc(s_const, 1)
            nc.gpsimd.memset(kpad[:, 0:P, :], 0.0).then_inc(s_const, 1)

            def scatter(layer, g):
                q = lg_of(layer, g)
                pool.wait_ge(s_route, q + 1)
                for t in range(TG):
                    for k in range(TOP_K):
                        i = t * TOP_K + k
                        uses = q * (TG * TOP_K // SC_SEMS) + i // SC_SEMS
                        if uses:
                            pool.wait_ge(s_scat[i % SC_SEMS], 16 * uses)
                        pool.indirect_dma_start(
                            out=slot_x[g],
                            out_offset=bass.IndirectOffsetOnAxis(ap=slots[:, q, k, t:t + 1].bitcast(U32), axis=0),
                            in_=xhl[:, g * TG + t, :, :].rearrange("p s c -> p (s c)"), in_offset=None).then_inc(s_scat[i % SC_SEMS], 16)

            def gather(layer, g):
                q = lg_of(layer, g)
                for u in range(YS_RING):
                    pool.wait_ge(s_yst[u], 16 * len([n for n in range((q + 1) * ST) if n % YS_RING == u]))
                for t in range(TG):
                    n = q * TG + t
                    if n >= YG_RING:
                        pool.wait_ge(s_comb, n - YG_RING + 1)
                    for k in range(TOP_K):
                        pool.indirect_dma_start(
                            out=yg[:, n % YG_RING, k, :], out_offset=None, in_=slot_y[layer][g],
                            in_offset=bass.IndirectOffsetOnAxis(ap=slots[:, q, k, t:t + 1].bitcast(U32), axis=0),
                        ).then_inc(s_yg[k][n % YG_RING], 16)

            pool.wait_ge(s_wmax, 1)
            nc.gpsimd.partition_all_reduce(wmax[:, :], wsc[:, 0:2], P, RMAX).then_inc(s_wall, 1)
            pool.wait_ge(s_zfill, 16 * G)
            scatter(0, 0)
            scatter(0, 1)
            gather(0, 0)
            gather(0, 1)
            scatter(1, 0)
            scatter(1, 1)
            gather(1, 0)
            gather(1, 1)

        @block.scalar
        def _(act):
            act.dma_start(ldt, log_dt.rearrange("(d a) -> d a", a=1)).then_inc(s_s4, 16)
            act.dma_start(sbt, s4_b).then_inc(s_s4, 16)
            act.dma_start(sct, s4_c).then_inc(s_s4, 16)
            act.wait_ge(s_zero, 1)
            for g in range(G):
                act.dma_start(slot_x[g].rearrange("(t p) c -> p t c", p=P),
                              zero16.rearrange("p (a c) -> p a c", a=1).to_broadcast([P, ST, 2 * D])).then_inc(s_zfill, 16)
            act.dma_start(b1s[:, :].rearrange("p (e k) -> p e k", e=E), b1.rearrange("e (p k) -> p e k", k=HC)).then_inc(s_b1, 16)
            act.dma_start(ds4[:, :], s4_d.rearrange("(a c) -> a c", a=1).to_broadcast([P, D])).then_inc(s_d, 16)
            act.dma_start(b2rep[:, :], b2.rearrange("(a e) c -> a (e c)", a=1).to_broadcast([P, E * D])).then_inc(s_b2, 16)

            def gate_copies(layer, g):
                q = lg_of(layer, g)
                for t in range(TG):
                    n = q * TG + t
                    act.wait_ge(s_xnt, n + 1)
                    if n >= 2:
                        act.wait_ge(s_gate, n - 1)
                    nc.scalar.activation(xnt[:, n % 2, :], CBK[n % 2][:, 0:P], ACT.Copy).then_inc(s_xntc, 1)

            def router_exps(layer, g):
                q = lg_of(layer, g)
                act.wait_ge(s_rsub, 2 * q + 1)
                nc.scalar.activation(sc[:, :, :], lg[:, :, :], ACT.Exp).then_inc(s_rexp, 1)
                act.wait_ge(s_rsub, 2 * q + 2)
                nc.scalar.activation(m2[:, :], mt[:, :], ACT.Exp).then_inc(s_rexp, 1)

            def reversed_copies(g):
                for i in range(TG // 2):
                    n = g * (TG // 2) + i
                    act.wait_ge(s_rev, n + 1)
                    nc.scalar.activation(xhl[:, 2 * n:2 * n + 2, :, :].rearrange("p t s c -> p (t s c)"),
                                         CBK[n % 2][:, :], ACT.Copy).then_inc(s_revc, 1)

            def weights_high():
                act.wait_ge(s_kin, 1)
                for e in range(E):
                    dst = w1hl[:, e * 1024:e * 1024 + 512].rearrange("p (k q) -> p k q", k=HC)
                    src = w1st[:, e * HID:(e + 1) * HID].rearrange("p (q k) -> p k q", k=HC)
                    nc.scalar.activation(dst, src, ACT.Copy, scale=wsc[:, 2:3]).then_inc(s_wh, 1)
                w2v = w2hl[:, :].rearrange("p (e s h) -> p e s h", e=E, s=2)
                nc.scalar.activation(w2v[:, :, 0, :], w2st.rearrange("p (e h) -> p e h", e=E), ACT.Copy,
                                     scale=wsc[:, 3:4]).then_inc(s_wh, 1)

            def kernel_powers():
                act.wait_ge(s_kt, 2)
                for n in range(N_STATE):
                    if n >= 4:
                        act.wait_ge(s_kacc, n - 3)
                    nc.scalar.activation(kexp[n % 4], kramp, ACT.Exp, scale=loga[:, n:n + 1]).then_inc(s_kexp, 1)

            def experts(layer, g):
                base = lg_of(layer, g) * ST

                def copy_xt(n, u):
                    act.wait_ge(s_xt, n + 1)
                    if not isinstance(n, int) or n >= 2:
                        act.wait_ge(s_h, n - 1)
                    nc.scalar.activation(xt[:, u % 2, :], XB[u % 2][:, 0:P].bitcast(F16), ACT.Copy).then_inc(s_xtc, 1)

                def relu(n, u):
                    e = act.value_load(etab[0:1, bass.ds(n, 1)], min_val=0, max_val=E - 1)
                    act.wait_ge(s_h, n + 1)
                    if not isinstance(n, int) or n >= 2:
                        act.wait_ge(s_hl, n - 1)
                    for k in range(HC):
                        r = nc.scalar.activation(hr[:, u % 2, k * P:(k + 1) * P], HB[u % 2][:, k * P:(k + 1) * P],
                                                 ACT.Relu, bias=b1s[:, bass.ds(e * HC + k, 1)])
                    r.then_inc(s_relu, 1)

                copy_xt(base, base % 4)

                def step(n, u):
                    if not (isinstance(n, int) and n == base + ST - 1):
                        copy_xt(n + 1, (u + 1) % 4)
                    relu(n, u)
                run_steps(act, base, base + ST - 1, 4, 3, step)
                step(base + ST - 1, (base + ST - 1) % 4)

            act.wait_ge(s_s4, 48)
            nc.scalar.activation(dtt, ldt, ACT.Exp).then_inc(s_ac, 1)
            act.wait_ge(s_kt, 1)
            nc.scalar.activation(th, dta, ACT.Tanh, scale=0.5).then_inc(s_ac, 1)
            gate_copies(0, 0)
            router_exps(0, 0)
            weights_high()
            gate_copies(0, 1)
            router_exps(0, 1)
            kernel_powers()
            experts(0, 0)
            experts(0, 1)
            for g in range(G):
                reversed_copies(g)
                gate_copies(1, g)
                router_exps(1, g)
            experts(1, 0)
            experts(1, 1)

        @block.vector
        def _(dve):
            V = nc.vector
            done = [0]

            def link(ins):
                done[0] += 1
                ins.then_inc(s_chain, 1)
                dve.wait_ge(s_chain, done[0])

            norm_n = [0]

            def normalise(tiles, wait_input=None, wait_place=None, skip=False):
                for i, t in enumerate(tiles):
                    if wait_input:
                        wait_input(t)
                    ins = V.bn_stats(st6[:, i, :], xa[:, t, :])
                link(ins)
                for i, t in enumerate(tiles):
                    ins = V.bn_aggr(mv[:, i, :], st6[:, i, :])
                link(ins)
                mean, var = mv[:, :, 0], mv[:, :, 1]
                link(V.tensor_scalar(nt1[:, :], var, EPS, None, ALU.add))
                link(V.tensor_scalar(nv[:, :], nt1[:, :], -0.5, None, ALU.mult))
                link(V.tensor_scalar(rstd[:, :].bitcast(I32), nt1[:, :].bitcast(I32), -0.5, float(0x5F3759DF), ALU.mult, ALU.add))
                for _ in range(3):
                    link(V.tensor_tensor(nt1[:, :], rstd[:, :], nv[:, :], ALU.mult))
                    link(V.tensor_tensor(nt1[:, :], nt1[:, :], rstd[:, :], ALU.mult))
                    link(V.scalar_tensor_tensor(rstd[:, :], nt1[:, :], 1.5, rstd[:, :], ALU.add, ALU.mult))
                for i, t in enumerate(tiles):
                    n = norm_n[0]
                    norm_n[0] += 1
                    r = n % XN_RING
                    if wait_place:
                        wait_place()
                    V.tensor_scalar(xn[:, r, :], xa[:, t, :], mv[:, i, 0:1], rstd[:, i:i + 1],
                                    ALU.subtract, ALU.mult).then_inc(s_xn, 1)
                    dve.wait_ge(s_xn, n + 1)
                    link(V.tensor_copy(xhl[:, t, 0, :], xn[:, r, :]))
                    V.tensor_tensor(xhl[:, t, 1, :], xn[:, r, :], xhl[:, t, 0, :], ALU.subtract).then_inc(s_xl, 1)
                    if skip:
                        dve.wait_ge(s_xl, n + 1)
                        link(V.tensor_tensor(xn[:, r, :], xn[:, r, :], ds4[:, :], ALU.mult))
                        link(V.tensor_tensor(xa[:, t, :], xa[:, t, :], xn[:, r, :], ALU.add))

            gate_n = [0]

            def x_loaded(t):
                if t % (NT // 4) == 0:
                    dve.wait_ge(s_x[t // (NT // 4)], 16)

            def xn_place():
                m = gate_n[0]
                gate_n[0] += 1
                if m >= XN_RING:
                    dve.wait_ge(s_xnt, m - XN_RING + 1)

            def bc_e(a):
                return a.rearrange("p (t a) -> p t a", a=1).to_broadcast([P, TG, E])

            def bc_t(a):
                return a.rearrange("p (a e) -> p a e", a=1).to_broadcast([P, TG, E])

            def route(layer, g):
                q = lg_of(layer, g)
                dve.wait_ge(s_gate, (q + 1) * TG)
                ins = V.tensor_tensor(lg[:, :, :], LG[:, 0:TE].rearrange("p (t e) -> p t e", e=E), bc_t(bgs[:, :]), ALU.add)
                ins.then_inc(s_logit, 1)
                dve.wait_ge(s_logit, q + 1)
                link(V.tensor_reduce(m1[:, :], lg[:, :, :], AX.X, ALU.max))
                V.tensor_tensor(lg[:, :, :], lg[:, :, :], bc_e(m1[:, :]), ALU.subtract).then_inc(s_rsub, 1)
                dve.wait_ge(s_rexp, 2 * q + 1)
                link(V.tensor_reduce(m1[:, :], sc[:, :, :], AX.X, ALU.add))
                link(V.reciprocal(m2[:, :], m1[:, :]))
                link(V.tensor_tensor(sc[:, :, :], sc[:, :, :], bc_e(m2[:, :]), ALU.mult))
                for k, m in ((0, m1), (1, m2)):
                    link(V.tensor_reduce(m[:, :], sc[:, :, :], AX.X, ALU.max))
                    link(V.tensor_tensor(eq[:, :, :], sc[:, :, :], bc_e(m[:, :]), ALU.is_equal))
                    link(V.tensor_tensor(eq[:, :, :], eq[:, :, :], bc_t(prio[:, :]), ALU.mult))
                    link(V.tensor_reduce(mt[:, :], eq[:, :, :], AX.X, ALU.max))
                    link(V.tensor_tensor(oh[k][:, :, :], eq[:, :, :], bc_e(mt[:, :]), ALU.is_equal))
                    if k == 0:
                        link(V.scalar_tensor_tensor(sc[:, :, :], oh[0][:, :, :], -2.0, sc[:, :, :], ALU.mult, ALU.add))
                V.tensor_tensor(ohs[:, :, :], oh[0][:, :, :], oh[1][:, :, :], ALU.add).then_inc(s_oh, 1)
                V.tensor_tensor(mt[:, :], m2[:, :], m1[:, :], ALU.subtract).then_inc(s_rsub, 1)
                dve.wait_ge(s_rexp, 2 * q + 2)
                link(V.tensor_scalar(m1[:, :], m2[:, :], 1.0, None, ALU.add))
                link(V.reciprocal(mt[:, :], m1[:, :]))
                link(V.tensor_scalar(prob[:, q, 0, :], mt[:, :], 0.5, None, ALU.mult))
                link(V.tensor_tensor(prob[:, q, 1, :], prob[:, q, 0, :], m2[:, :], ALU.mult))
                dve.wait_ge(s_pre, q + 1)
                link(V.tensor_copy(tot[:, :, :].rearrange("p e t -> p t e"),
                                   CBK[0][:, TE:2 * TE].rearrange("p (t e) -> p t e", e=E)))
                link(V.tensor_tensor_scan(cum[:, :, :].rearrange("p e t -> p (e t)"), segm[:, :, :].rearrange("p e t -> p (e t)"),
                                          tot[:, :, :].rearrange("p e t -> p (e t)"), 0.0, ALU.mult, ALU.add))
                link(V.tensor_scalar(cnti[:, :], cum[:, :, TG - 1], float(P - 1), None, ALU.add))
                link(V.tensor_scalar(cnti[:, :], cnti[:, :], -P, None, ALU.bitwise_and))
                link(V.tensor_copy(cnt[:, :], cnti[:, :]))
                link(V.tensor_tensor_scan(ends[:, :], one8[:, :], cnt[:, :], 0.0, ALU.mult, ALU.add))
                link(V.tensor_tensor(cnt[:, :], ends[:, :], cnt[:, :], ALU.subtract))
                link(V.tensor_tensor(cum[:, :, :], cum[:, :, :], tot[:, :, :], ALU.subtract))
                link(V.tensor_tensor(pos[:, :, :], cum[:, :, :].rearrange("p e t -> p t e"), bc_t(cnt[:, :]), ALU.add))
                link(V.tensor_tensor(pos[:, :, :], CBK[0][:, 0:TE].rearrange("p (t e) -> p t e", e=E), pos[:, :, :], ALU.add))
                for k in range(TOP_K):
                    link(V.tensor_tensor(eq[:, :, :], oh[k][:, :, :], pos[:, :, :], ALU.mult))
                    link(V.tensor_reduce(slotf[:, :], eq[:, :, :], AX.X, ALU.add))
                    link(V.tensor_copy(slots[:, q, k, :], slotf[:, :]))
                link(V.tensor_tensor(et1, ends[0:1, :].rearrange("p (a e) -> p a e", a=1).to_broadcast([1, ST, E]),
                                     tstart[:, :, :], ALU.is_le))
                link(V.tensor_reduce(et2[:, :], et1, AX.X, ALU.add))
                V.tensor_scalar(etab[:, q * ST:(q + 1) * ST], et2[:, :], float(E - 1), None, ALU.min).then_inc(s_route, 1)
                dve.wait_ge(s_route, q + 1)

            def weight_scales():
                dve.wait_ge(s_w1, 16)
                link(V.tensor_reduce(wsc[:, 0:1], w1st, AX.X, ALU.max, apply_absolute_value=True))
                dve.wait_ge(s_b1, 16)
                link(V.tensor_reduce(wsc[:, 1:2], b1s[:, :], AX.X, ALU.max, apply_absolute_value=True))
                link(V.tensor_tensor(wsc[:, 0:1], wsc[:, 0:1], wsc[:, 1:2], ALU.max))
                dve.wait_ge(s_w2, 16)
                link(V.tensor_reduce(wsc[:, 1:2], w2st, AX.X, ALU.max, apply_absolute_value=True))
                V.tensor_scalar(wsc[:, 0:2], wsc[:, 0:2], 1e-30, None, ALU.max).then_inc(s_wmax, 1)
                dve.wait_ge(s_wall, 1)
                link(V.tensor_scalar(wsc[:, 2:4].bitcast(I32), wmax[:, 0:2].bitcast(I32), EXPONENT, EXPONENT,
                                     ALU.bitwise_and, ALU.bitwise_xor))
                link(V.tensor_scalar(wsc[:, 4:6].bitcast(I32), wmax[:, 0:2].bitcast(I32), EXPONENT, None, ALU.bitwise_and))
                link(V.tensor_scalar(wsc[:, 4:6], wsc[:, 4:6], 0.5, None, ALU.mult))
                link(V.tensor_tensor(wsc[:, 6:7], wsc[:, 4:5], wsc[:, 5:6], ALU.mult))
                V.tensor_scalar(b1s[:, :], b1s[:, :], wsc[:, 2:3], None, ALU.mult).then_inc(s_kin, 1)

            def weights_low():
                dve.wait_ge(s_wh, E + 1)
                for e in range(E):
                    o = e * 1024
                    V.scalar_tensor_tensor(
                        w1hl[:, o + 512:o + 1024].rearrange("p (k q) -> p k q", k=HC),
                        w1st[:, e * HID:(e + 1) * HID].rearrange("p (q k) -> p k q", k=HC), wsc[:, 2:3],
                        w1hl[:, o:o + 512].rearrange("p (k q) -> p k q", k=HC), ALU.mult, ALU.subtract)
                w2v = w2hl[:, :].rearrange("p (e s h) -> p e s h", e=E, s=2)
                dve.wait_ge(s_kin, 1)
                V.scalar_tensor_tensor(w2v[:, :, 1, :], w2st.rearrange("p (e h) -> p e h", e=E), wsc[:, 3:4],
                                       w2v[:, :, 0, :], ALU.mult, ALU.subtract).then_inc(s_wready, 1)

            def kernel_arguments():
                dve.wait_ge(s_const, 13)
                dve.wait_ge(s_ac, 1)
                V.tensor_scalar(dta, nar, dtt, -0.5, ALU.mult, ALU.mult).then_inc(s_kt, 1)
                dve.wait_ge(s_kt, 1)
                link(V.tensor_scalar(loga, dta, LOG_FLOOR, None, ALU.max))
                link(V.reciprocal(rn, nar))
                dve.wait_ge(s_ac, 2)
                link(V.tensor_scalar(rden, th, -1.0, 1.0, ALU.mult, ALU.add))
                link(V.reciprocal(kw, rden))
                link(V.scalar_tensor_tensor(rden, th, -4.0, kw, ALU.mult, ALU.mult))
                link(V.tensor_tensor(rden, rden, rn, ALU.mult))
                link(V.tensor_tensor(rden, rden, sbt, ALU.mult))
                V.tensor_tensor(kw, rden, sct, ALU.mult).then_inc(s_kt, 1)
                dve.wait_ge(s_kt, 2)

            def kernel_sum():
                for n in range(N_STATE):
                    dve.wait_ge(s_kexp, n + 1)
                    if n == 0:
                        ins = V.tensor_scalar(kacc, kexp[0], kw[:, 0:1], None, ALU.mult)
                    else:
                        ins = V.scalar_tensor_tensor(kacc, kexp[n % 4], kw[:, n:n + 1], kacc, ALU.mult, ALU.add)
                    ins.then_inc(s_kacc, 1)
                    dve.wait_ge(s_kacc, n + 1)
                link(V.tensor_reduce(kmx, kacc, AX.X, ALU.max, apply_absolute_value=True))
                link(V.tensor_scalar(kmx, kmx, 1e-30, None, ALU.max))
                link(V.tensor_scalar(kal.bitcast(I32), kmx.bitcast(I32), EXPONENT, EXPONENT, ALU.bitwise_and, ALU.bitwise_xor))
                link(V.tensor_scalar(kiv.bitcast(I32), kmx.bitcast(I32), EXPONENT, None, ALU.bitwise_and))
                link(V.tensor_scalar(kiv, kiv, 0.5, None, ALU.mult))
                V.tensor_scalar(kdiag, ident[:, :], kiv, None, ALU.mult).then_inc(s_kdiag, 1)
                link(V.tensor_scalar(kpad[:, P:, 0], kacc, kal, None, ALU.mult))
                V.scalar_tensor_tensor(kpad[:, P:, 1], kacc, kal, kpad[:, P:, 0], ALU.mult, ALU.subtract).then_inc(s_kpad, 1)
                dve.wait_ge(s_kinv, 1)
                V.tensor_copy(kinv[:, :], CBK[1][:, 0:D]).then_inc(s_kinvc, 1)

            def experts(layer, g):
                base = lg_of(layer, g) * ST

                def split(n, u):
                    dve.wait_ge(s_relu, n + 1)
                    if not isinstance(n, int) or n >= 2:
                        dve.wait_ge(s_y, n - 1)
                    V.tensor_copy(hh[:, u % 2, :], hr[:, u % 2, :]).then_inc(s_hh, 1)
                    dve.wait_ge(s_hh, n + 1)
                    V.tensor_tensor(hl[:, u % 2, :], hr[:, u % 2, :], hh[:, u % 2, :], ALU.subtract).then_inc(s_hl, 1)

                def output(n, u):
                    e = dve.value_load(etab[0:1, bass.ds(n, 1)], min_val=0, max_val=E - 1)
                    dve.wait_ge(s_y, n + 1)
                    if not isinstance(n, int) or n >= YS_RING:
                        dve.wait_ge(s_yst[u], (n // YS_RING) * 16 if isinstance(n, int) else (n - u) * (16 // YS_RING))
                    V.scalar_tensor_tensor(ysb[:, u, :], YB[u % 2][:, 0:D], wsc[:, 6:7], b2rep[:, bass.ds(e * D, D)],
                                           ALU.mult, ALU.add).then_inc(s_yc, 1)

                def step(n, u):
                    split(n, u)
                    if not isinstance(n, int) or n >= base + 2:
                        output(n - 2, (u - 2) % 4)
                run_steps(dve, base, base + ST, 4, base + 6, step)
                for n in (base + ST - 2, base + ST - 1):
                    output(n, n % 4)

            def combine(layer, g):
                q = lg_of(layer, g)
                for t in range(TG):
                    n = q * TG + t
                    tile = xa[:, g * TG + t, :]
                    for k in range(TOP_K):
                        dve.wait_ge(s_yg[k][n % YG_RING], 16 * (n // YG_RING + 1))
                    link(V.scalar_tensor_tensor(tile, yg[:, n % YG_RING, 0, :], prob[:, q, 0, t:t + 1], tile, ALU.mult, ALU.add))
                    ins = V.scalar_tensor_tensor(tile, yg[:, n % YG_RING, 1, :], prob[:, q, 1, t:t + 1], tile, ALU.mult, ALU.add)
                    ins.then_inc(s_comb, 1)
                    dve.wait_ge(s_comb, n + 1)

            def conv_input(g):
                dve.wait_ge(s_d, 16)
                for k in range(SC_SEMS):
                    dve.wait_ge(s_scat[k], 16 * G * (TG * TOP_K // SC_SEMS))
                normalise(range(g * TG, (g + 1) * TG), skip=True)

            cv_n = [0]
            cvt = hr[:, :, :].rearrange("p a b -> p (a b)")

            def conv_output(g):
                for cb in conv_blocks(g):
                    n = cv_n[0]
                    cv_n[0] += 1
                    dve.wait_ge(s_cv, n + 1)
                    tmp = cvt[:, (n % 2) * 512:(n % 2) * 512 + 512].rearrange("p (t c) -> p t c", c=CB)
                    scale = kinv[:, cb * CB:(cb + 1) * CB].rearrange("p (a c) -> p a c", a=1).to_broadcast([P, TG, CB])
                    V.tensor_tensor(tmp, CBK[n % 2][:, :].rearrange("p (t c) -> p t c", c=CB), scale, ALU.mult).then_inc(s_cve, 1)
                    dve.wait_ge(s_cve, n + 1)
                    dst = xa[:, g * TG:(g + 1) * TG, cb * CB:(cb + 1) * CB]
                    link(V.tensor_tensor(dst, dst, tmp, ALU.add))

            kernel_arguments()
            normalise(range(0, TG), x_loaded, xn_place)
            dve.wait_ge(s_wg, 32)
            route(0, 0)
            weight_scales()
            normalise(range(TG, NT), x_loaded, xn_place)
            route(0, 1)
            weights_low()
            kernel_sum()
            dve.wait_ge(s_b2, 16)
            experts(0, 0)
            experts(0, 1)
            for g in range(G):
                combine(0, g)
                conv_input(g)
            for g in range(G):
                conv_output(g)
                normalise(range(g * TG, (g + 1) * TG), None, xn_place)
                route(1, g)
            experts(1, 0)
            experts(1, 1)
            combine(1, 0)
            combine(1, 1)

        @block.tensor
        def _(pe):
            def mm(o, a, b, start, stop):
                return nc.tensor.matmul(o, lhsT=a, rhs=b, start=start, stop=stop)

            def gate(layer, g):
                q = lg_of(layer, g)

                def product(n):
                    t = n - q * TG
                    pe.wait_ge(s_xntc, n + 1)
                    mm(LG[:, t * E:(t + 1) * E], xnt[:, n % 2, :], wgs[:, :], True, True).then_inc(s_gate, 1)

                if q:
                    pe.wait_ge(s_route, q)
                if layer:
                    pe.wait_ge(s_cve, (g + 1) * (D // CB))
                for t in range(TG):
                    n = q * TG + t
                    r = (n + (0 if layer == 0 else NT)) % XN_RING
                    pe.wait_ge(s_xn, n + 1 + (0 if layer == 0 else NT))
                    if n >= 2:
                        pe.wait_ge(s_xntc, n - 1)
                    nc.tensor.transpose(CBK[n % 2][:, 0:P], xn[:, r, :], ident[:, :]).then_inc(s_xnt, 1)
                    if t:
                        product(n - 1)
                product(q * TG + TG - 1)
                pe.wait_ge(s_oh, q + 1)
                ohf = ohs[:, :, :].rearrange("p t e -> p (t e)")
                mm(CBK[0][:, 0:TE], before16[:, :], ohf, True, True)
                mm(CBK[0][:, TE:2 * TE], ones16[:, :], ohf, True, True).then_inc(s_pre, 1)

            def experts(layer, g):
                base = lg_of(layer, g) * ST
                pe.wait_ge(s_route, lg_of(layer, g) + 1)

                def front(n, u):
                    pe.wait_ge(s_xs[u], (n // XS_RING + 1) * 16 if isinstance(n, int) else (n - u + XS_RING) * (16 // XS_RING))
                    if not isinstance(n, int) or n >= 2:
                        pe.wait_ge(s_xtc, n - 1)
                    b = XB[u % 2][:, 0:P].bitcast(F16)
                    nc.tensor.transpose(b[:, 0:P], xs[:, u, 0:P], ident16[:, :])
                    nc.tensor.transpose(b[:, P:2 * P], xs[:, u, P:2 * P], ident16[:, :]).then_inc(s_xt, 1)

                def hidden(n, u):
                    e = pe.value_load(etab[0:1, bass.ds(n, 1)], min_val=0, max_val=E - 1)
                    pe.wait_ge(s_xtc, n + 1)
                    if not isinstance(n, int) or n >= 2:
                        pe.wait_ge(s_relu, n - 1)
                    xh, xl = xt[:, u % 2, 0:P], xt[:, u % 2, P:2 * P]
                    for k in range(HC):
                        o = HB[u % 2][:, k * P:(k + 1) * P]
                        wh = w1hl[:, bass.ds(e * 1024 + k * P, P)]
                        wl = w1hl[:, bass.ds(e * 1024 + 512 + k * P, P)]
                        mm(o, wh, xh, True, False)
                        mm(o, wh, xl, False, False)
                        last = mm(o, wl, xh, False, True)
                    last.then_inc(s_h, 1)

                def output(n, u):
                    e = pe.value_load(etab[0:1, bass.ds(n, 1)], min_val=0, max_val=E - 1)
                    pe.wait_ge(s_hl, n + 1)
                    if not isinstance(n, int) or n >= 2:
                        pe.wait_ge(s_yc, n - 1)
                    o = YB[u % 2][:, 0:D]
                    for k in range(HC):
                        ah, al = hh[:, u % 2, k * P:(k + 1) * P], hl[:, u % 2, k * P:(k + 1) * P]
                        wh = w2hl[:, bass.ds(e * 1024 + k * P, P)]
                        wl = w2hl[:, bass.ds(e * 1024 + 512 + k * P, P)]
                        mm(o, ah, wh, k == 0, False)
                        mm(o, ah, wl, False, False)
                        last = mm(o, al, wh, False, k == HC - 1)
                    last.then_inc(s_y, 1)

                front(base, base % 4)

                def step(n, u):
                    if not (isinstance(n, int) and n == base + ST - 1):
                        front(n + 1, (u + 1) % 4)
                    hidden(n, u)
                    if not isinstance(n, int) or n >= base + 2:
                        output(n - 2, (u - 2) % 4)
                run_steps(pe, base, base + ST - 1, 4, max(base + 2, 4), step)
                step(base + ST - 1, (base + ST - 1) % 4)
                for n in (base + ST - 2, base + ST - 1):
                    output(n, n % 4)

            def reverse(g):
                if g:
                    pe.wait_ge(s_route, LAYERS * G - G + g)
                for i in range(TG // 2):
                    n = g * (TG // 2) + i
                    t = 2 * n
                    pe.wait_ge(s_xl, NT + t + 2)
                    if n >= 2:
                        pe.wait_ge(s_revc, n - 1)
                    mm(CBK[n % 2][:, :], back16[:, :], xhl[:, t:t + 2, :, :].rearrange("p t s c -> p (t s c)"),
                       True, True).then_inc(s_rev, 1)
                pe.wait_ge(s_revc, (g + 1) * (TG // 2))

            def conv(g):
                for i, cb in enumerate(conv_blocks(g)):
                    n = g * (D // CB) + i
                    if i >= 2:
                        pe.wait_ge(s_cve, n - 1)
                    b = CBK[n % 2][:, :].rearrange("p (t c) -> p t c", c=CB)
                    for c in range(CB):
                        d = cb * CB + c
                        part = d // TC
                        if d % TC == 0 and g == 0:
                            pe.wait_ge(s_toep[part], 16)
                        if d == 0 and g:
                            pe.wait_ge(s_tagain, 16)
                        at = toeplitz_place(part, g) * TC + d % TC
                        th0, tl0 = toep[:, at, 0:2 * P:2], toep[:, at, 1:2 * P:2]
                        th1, tl1 = toep[:, at, 2 * P::2], toep[:, at, 2 * P + 1::2]
                        a, z = g * TG, (g + 1) * TG
                        xh, xl = xhl[:, a:z, 0, d], xhl[:, a:z, 1, d]
                        xh0, xl0 = xhl[:, a:z:2, 0, d], xhl[:, a:z:2, 1, d]
                        o, o1 = b[:, :, c], b[:, 1::2, c]
                        mm(o, th0, xh, True, False)
                        mm(o, th0, xl, False, False)
                        mm(o1, th1, xh0, False, False)
                        mm(o1, th1, xl0, False, False)
                        mm(o1, tl1, xh0, False, False)
                        last = mm(o, tl0, xh, False, True)
                    last.then_inc(s_cv, 1)

            pe.wait_ge(s_const, 13)
            pe.wait_ge(s_wg, 32)
            gate(0, 0)
            gate(0, 1)
            pe.wait_ge(s_kdiag, 1)
            mm(CBK[1][:, 0:D], onesf, kdiag, True, True).then_inc(s_kinv, 1)
            pe.wait_ge(s_wready, 1)
            experts(0, 0)
            experts(0, 1)
            pe.wait_ge(s_kinvc, 1)
            for g in range(G):
                reverse(g)
                conv(g)
                gate(1, g)
            experts(1, 0)
            experts(1, 1)


_INS = ['L0_attn_x', 'L0_attn_log_dt', 'L0_attn_B', 'L0_attn_C', 'L0_attn_D', 'L0_ffn_W1', 'L0_ffn_b1',
        'L0_ffn_W2', 'L0_ffn_b2', 'L0_ffn_Wg', 'L0_ffn_bg']


def kernel(**inputs):
    import numpy as _np
    import concourse.bacc as _bacc
    from concourse import mybir as _mybir
    from concourse.bass_utils import run_bass_kernel_spmd as _run

    nc = _bacc.Bacc("TRN2", target_bir_lowering=False, num_devices=1)
    arrays, args = {}, []
    for name in _INS:
        a = _np.ascontiguousarray(inputs[name])
        arrays[f"in_{name}_dram"] = a
        args.append(nc.dram_tensor(f"in_{name}_dram", a.shape, _mybir.dt.from_np(a.dtype), kind="ExternalInput").ap())
    args.append(nc.dram_tensor("out_0_dram", (BATCH, LENGTH, D), _mybir.dt.float32, kind="ExternalOutput").ap())
    macaron_kernel(nc, *args)
    r = _run(nc, [arrays], core_ids=[0])
    return r.results[0]["out_0_dram"]
```

```python
import concourse.bass as bass
from concourse import mybir
from contextlib import ExitStack

P = 128
BATCH, LENGTH, D = 16, 256, 128
N_STATE = 64
E, HID, TOP_K = 8, 512, 2
HC = HID // P
NT = BATCH * LENGTH // P
G = 2
TG = NT // G
OCTET = 8
ST = -(-((TG * P * TOP_K - E) // P + E) // OCTET) * OCTET
LAYERS = 2
EPS = 1e-5
LOG_FLOOR = -23.025850929940457
XS_RING, YS_RING, XN_RING, YG_RING = 4, 4, 4, 4
KEXP_RING = 4
TINY = 1e-15
SC_SEMS = 8
EXPONENT = 0x7F800000
KPAD = LENGTH + P
CB = 32
TC = 16
T_PARTS = D // TC
T_PLACES = T_PARTS - 1


def toeplitz_place(part, g):
    return part if part not in (0, T_PARTS - 1) else (0 if part else (0 if g == 0 else 2))


def conv_blocks(g):
    return [0, 1, 2, 3] if g == 0 else [1, 2, 3, 0]


ROUNDS = ST // OCTET


def run_octets(eng, base, octet, peel_last=False):
    octet(base, 0, True, False)
    with eng.Fori(1, ROUNDS - 1 if peel_last else ROUNDS) as r:
        octet(r * OCTET + base, r, False, False)
    if peel_last:
        octet(base + ST - OCTET, ROUNDS - 1, False, True)


NORMS = [("router", 0, 0), ("router", 0, 1), ("conv", 1, 0), ("router", 1, 0), ("conv", 1, 1), ("router", 1, 1)]


def norm_base(kind, layer, g):
    return NORMS.index((kind, layer, g)) * TG


def first(n, count):
    return isinstance(n, int) and n < count


def macaron_kernel(nc, x, log_dt, s4_b, s4_c, s4_d, w1, b1, w2, b2, wg, bg, out):
    F32, F16, BF16, I32, U32 = mybir.dt.float32, mybir.dt.float16, mybir.dt.bfloat16, mybir.dt.int32, mybir.dt.uint32
    ALU, ACT, AX = mybir.AluOpType, mybir.ActivationFunctionType, mybir.AxisListType
    RMAX = bass.bass_isa.ReduceOp.max

    with ExitStack() as ctx:
        def sb(name, shape, dt=F32):
            return ctx.enter_context(nc.sbuf_tensor(name, shape, dt))

        def sem(name):
            return ctx.enter_context(nc.semaphore(name))

        def sems(name, n):
            return [sem(f"{name}{i}") for i in range(n)]

        slot_x = [nc.dram_tensor(f"slot_x{g}", [ST * P, 2 * D], F16, kind="Internal").ap() for g in range(G)]
        slot_y = [[nc.dram_tensor(f"slot_y{l}{g}", [ST * P, D], F32, kind="Internal").ap()
                   for g in range(G)] for l in range(LAYERS)]
        kern_d = nc.dram_tensor("kern_d", [P, 2 * KPAD], F16, kind="Internal").ap()

        xa = sb("xa", [P, NT, D])
        xhl = sb("xhl", [P, NT, 2, D], F16)
        w1hl = sb("w1hl", [P, E * 2 * HC * P], F16)
        w2hl = sb("w2hl", [P, E * 2 * HC * D], F16)
        toep = sb("toep", [P, T_PLACES * TC, 2 * LENGTH], F16)
        b1rows = sb("b1rows", [P, HID], F16)
        b2rows = sb("b2rows", [P, E * D], BF16)
        sel = sb("sel", [P, E], F16)
        wgs = sb("wgs", [P, E])
        bgs = sb("bgs", [P, E])
        ident = sb("ident", [P, P])
        ident16 = sb("ident16", [P, P], F16)
        before16 = sb("before16", [P, P], F16)
        ones16 = sb("ones16", [P, P], F16)
        back16 = sb("back16", [P, P], F16)
        kinv = sb("kinv", [P, D])
        wsc = sb("wsc", [P, 8])
        wmax = sb("wmax", [P, 2])
        xs = sb("xs", [P, XS_RING, 2 * D], F16)
        xt = sb("xt", [P, 2, 2 * P], F16)
        hsplit = sb("hsplit", [P, 4, HID], F16)
        hh, hl = hsplit[:, 0:2, :], hsplit[:, 2:4, :]
        ysb = sb("ysb", [P, YS_RING, D])
        yg = sb("yg", [P, YG_RING, TOP_K, D])
        xn = sb("xn", [P, XN_RING, D])
        xnt = sb("xnt", [P, 2, P])
        TE = TG * E
        mv = sb("mv", [P, TG, 2])
        st6 = sb("st6", [P, TG, 6])
        rstd = sb("rstd", [P, TG])
        lg = sb("lg", [P, TG, E])
        sc = sb("sc", [P, TG, E])
        eq = sb("eq", [P, TG, E])
        oh = [sb(f"oh{k}", [P, TG, E], F16) for k in range(TOP_K)]
        ohs = sb("ohs", [P, TG, E], F16)
        m1 = sb("m1", [P, TG])
        m2 = sb("m2", [P, TG])
        mt = sb("mt", [P, TG])
        nv, nt1 = m1, mt
        tot = sb("tot", [P, E, TG])
        cum = sb("cum", [P, E, TG])
        pos = sb("pos", [P, TG, E])
        cnt = sb("cnt", [P, E])
        cnti = sb("cnti", [P, E], I32)
        ends = sb("ends", [P, E])
        slotf = sb("slotf", [P, TG])
        slots = sb("slots", [P, LAYERS * G, TOP_K, TG], I32)
        prob = sb("prob", [P, LAYERS * G, TOP_K, TG])
        et1 = xn[:, :, :].rearrange("p a b -> p (a b)")[0:1, 0:ST * E].rearrange("p (j e) -> p j e", e=E)
        et2 = sb("et2", [1, ST])
        etab = sb("etab", [1, LAYERS * G * ST], I32)
        prio = sb("prio", [P, E])
        segm = sb("segm", [P, E, TG], F16)
        one8 = sb("one8", [P, E])
        tstart = sb("tstart", [1, ST, E], F16)
        zero16 = xt[:, 0, :]
        tview = toep[:, :, :].rearrange("p a b -> p (a b)").bitcast(F32)
        used = [0]

        def scratch(n):
            used[0] += n
            assert used[0] <= T_PLACES * TC * LENGTH
            return tview[:, used[0] - n:used[0]]

        w1st, w2st = scratch(E * HID), scratch(E * HID)
        kramp = scratch(LENGTH)
        kexp = [scratch(LENGTH) for _ in range(KEXP_RING)]
        kacc = scratch(LENGTH)
        kpad = scratch(KPAD).bitcast(F16).rearrange("p (k s) -> p k s", s=2)
        nar, dta, loga, th, rden, rn, kw, sbt, sct = (scratch(N_STATE) for _ in range(9))
        ldt, dtt, kmx, kal, kiv = (scratch(1) for _ in range(5))
        kdiag = scratch(P)
        onesf = scratch(P)
        dcol = scratch(1)
        b1f, b2f = scratch(HID), scratch(E * D)

        bank = [ctx.enter_context(nc.psum_tensor(f"bank{i}", [P, 512], F32)) for i in range(8)]
        HB, XB, YB, CBK = bank[0:2], bank[2:4], bank[4:6], bank[6:8]
        LG = XB[0]

        s_x = sems("s_x", 4)
        s_w1, s_w2, s_b1, s_b2, s_wg, s_s4 = (sem(n) for n in ("s_w1", "s_w2", "s_b1", "s_b2", "s_wg", "s_s4"))
        s_bzero = sem("s_bzero")
        s_zero = sem("s_zero")
        s_zfill = sem("s_zfill")
        s_const = sem("s_const")
        s_id = sem("s_id")
        s_chain = sem("s_chain")
        s_ac = sem("s_ac")
        s_wmax = sem("s_wmax")
        s_wall = sem("s_wall")
        s_wh = sem("s_wh")
        s_wready = sem("s_wready")
        s_kin = sem("s_kin")
        s_kt = sem("s_kt")
        s_kexp = sem("s_kexp")
        s_kacc = sem("s_kacc")
        s_kpad = sem("s_kpad")
        s_kst = sem("s_kst")
        s_kdiag = sem("s_kdiag")
        s_kinv = sem("s_kinv")
        s_kinvc = sem("s_kinvc")
        s_toep = sem("s_toep")
        s_tlast = sem("s_tlast")
        s_tagain = sem("s_tagain")
        s_xn = sem("s_xn")
        s_xh = sem("s_xh")
        s_xl = sem("s_xl")
        s_xnt = sem("s_xnt")
        s_xntc = sem("s_xntc")
        s_gate = sem("s_gate")
        s_logit = sem("s_logit")
        s_rsub = sem("s_rsub")
        s_rexp = sem("s_rexp")
        s_oh = sem("s_oh")
        s_pre = sem("s_pre")
        s_route = sem("s_route")
        s_scat = sems("s_scat", SC_SEMS)
        s_xs = sems("s_xs", XS_RING)
        s_xt = sem("s_xt")
        s_xtc = sem("s_xtc")
        s_h = sem("s_h")
        s_relu = sem("s_relu")
        s_hl = sem("s_hl")
        s_y = sem("s_y")
        s_yc = sem("s_yc")
        s_yst = sems("s_yst", YS_RING)
        s_yg = [sems(f"s_yg{k}", YG_RING) for k in range(TOP_K)]
        s_part = sem("s_part")
        s_comb = sem("s_comb")
        s_rev = sem("s_rev")
        s_revc = sem("s_revc")
        s_cv = sem("s_cv")
        s_cve = sem("s_cve")
        s_out = sem("s_out")

        x_t = x.rearrange("b (h p) c -> p (b h) c", p=P)
        out_t = out.rearrange("b (h p) c -> p (b h) c", p=P)
        lg_of = lambda layer, g: layer * G + g

        block = ctx.enter_context(nc.Block())

        @block.sync
        def _(sp):
            XQ = NT // 4
            sp.dma_start(xa[:, 0:XQ, :], x_t[:, 0:XQ, :]).then_inc(s_x[0], 16)
            sp.dma_start(xa[:, XQ:2 * XQ, :], x_t[:, XQ:2 * XQ, :]).then_inc(s_x[1], 16)
            sp.dma_start(wgs[:, :], wg).then_inc(s_wg, 16)
            sp.dma_start(bgs[:, :], bg.rearrange("(a e) -> a e", a=1).to_broadcast([P, E])).then_inc(s_wg, 16)
            sp.dma_start(w1st.rearrange("p (e h) -> p e h", e=E), w1.rearrange("e c h -> c e h")).then_inc(s_w1, 16)
            sp.dma_start(w2st.rearrange("p (e h) -> p e h", e=E),
                         w2.rearrange("e (p k) c -> p e (k c)", k=HC)).then_inc(s_w2, 16)
            sp.dma_start(xa[:, 2 * XQ:3 * XQ, :], x_t[:, 2 * XQ:3 * XQ, :]).then_inc(s_x[2], 16)
            sp.dma_start(xa[:, 3 * XQ:, :], x_t[:, 3 * XQ:, :]).then_inc(s_x[3], 16)

            def load_toeplitz(channel, count, place, signal):
                src = bass.AP(kern_d.tensor, 2, [[2, P], [2 * KPAD, P], [1, 2 * LENGTH]])
                sp.dma_start(toep[:, bass.ds(place, count), :], src[:, bass.ds(channel, count), :]).then_inc(signal, 16)

            TD = 4
            STORE_LAG = 6

            def expert_io(layer, g, toeplitz=False):
                base = lg_of(layer, g) * ST
                for k in range(SC_SEMS):
                    sp.wait_ge(s_scat[k], 16 * (lg_of(layer, g) + 1) * (TG * TOP_K // SC_SEMS))

                def load(n, u):
                    if not first(n, XS_RING):
                        sp.wait_ge(s_xt, n - (XS_RING - 1))
                    sp.dma_start(xs[:, u % XS_RING, :], slot_x[g][bass.ds((n - base) * P, P), :]).then_inc(s_xs[u % XS_RING], 16)

                def store(n, u):
                    sp.wait_ge(s_yc, n + 1)
                    sp.dma_start(slot_y[layer][g][bass.ds((n - base) * P, P), :],
                                 ysb[:, u % YS_RING, :]).then_inc(s_yst[u % YS_RING], 16)

                def octet(n0, r, start, end):
                    for u in range(OCTET):
                        load(n0 + u, u)
                        if not start or u >= STORE_LAG:
                            store(n0 + u - STORE_LAG, u - STORE_LAG)
                        if toeplitz and start and u == 2:
                            sp.wait_ge(s_kpad, 1)
                            sp.dma_start(kern_d, kpad.rearrange("p k s -> p (k s)")).then_inc(s_kst, 16)
                        if toeplitz and start and u == OCTET - 1:
                            sp.wait_ge(s_kst, 16)
                            sp.wait_ge(s_kinvc, 1)
                        if toeplitz and not start and u < OCTET - 1:
                            c = (r - 1) * (7 * TD) + u * TD
                            load_toeplitz(c, TD, c, s_toep)
                run_octets(sp, base, octet)
                for u in range(OCTET - STORE_LAG, OCTET):
                    store(base + ST - OCTET + u, u)

            expert_io(0, 0)
            expert_io(0, 1, toeplitz=True)
            sp.wait_ge(s_cv, 1)
            load_toeplitz(D - TC, TC, 0, s_tlast)
            sp.wait_ge(s_cv, D // CB + 1)
            load_toeplitz(0, TC, 2 * TC, s_tagain)
            for g in range(G):
                expert_io(1, g)
            for t in range(NT):
                sp.wait_ge(s_comb, NT + t + 1)
                sp.dma_start(out_t[:, t, :], xa[:, t, :]).then_inc(s_out, 16)
            sp.wait_ge(s_out, 16 * NT)

        @block.gpsimd
        def _(pool):
            done = [0]

            def link(ins):
                done[0] += 1
                ins.then_inc(s_id, 1)
                pool.wait_ge(s_id, done[0])

            nc.gpsimd.memset(zero16, 0.0).then_inc(s_zero, 1)
            nc.gpsimd.memset(b1f, 0.0).then_inc(s_bzero, 1)
            nc.gpsimd.memset(b2f, 0.0).then_inc(s_bzero, 1)
            link(nc.gpsimd.memset(ident[:, :], 0.0))
            nc.gpsimd.affine_select(out=ident[:, :], in_=ident[:, :], compare_op=ALU.not_equal, fill=1.0,
                                    base=0, pattern=[[-1, P]], channel_multiplier=1).then_inc(s_const, 1)
            link(nc.gpsimd.memset(ident16[:, :], 0.0))
            nc.gpsimd.affine_select(out=ident16[:, :], in_=ident16[:, :], compare_op=ALU.not_equal, fill=1.0,
                                    base=0, pattern=[[-1, P]], channel_multiplier=1).then_inc(s_const, 1)
            link(nc.gpsimd.memset(back16[:, :], 0.0))
            nc.gpsimd.affine_select(out=back16[:, :], in_=back16[:, :], compare_op=ALU.not_equal, fill=1.0,
                                    base=1 - P, pattern=[[1, P]], channel_multiplier=1).then_inc(s_const, 1)
            nc.gpsimd.memset(ones16[:, :], 1.0).then_inc(s_const, 1)
            nc.gpsimd.memset(onesf, 1.0).then_inc(s_const, 1)
            nc.gpsimd.memset(one8[:, :], 1.0).then_inc(s_const, 1)
            link(nc.gpsimd.memset(before16[:, :], 1.0))
            nc.gpsimd.affine_select(out=before16[:, :], in_=before16[:, :], compare_op=ALU.is_gt, fill=0.0,
                                    base=0, pattern=[[1, P]], channel_multiplier=-1).then_inc(s_const, 1)
            link(nc.gpsimd.memset(segm[:, :, :], 1.0))
            nc.gpsimd.memset(segm[:, :, 0:1], 0.0).then_inc(s_const, 1)
            nc.gpsimd.iota(prio[:, :], pattern=[[-1, E]], base=E, channel_multiplier=0,
                           allow_small_or_imprecise_dtypes=True).then_inc(s_const, 1)
            nc.gpsimd.iota(tstart[:, :, :], pattern=[[P, ST], [0, E]], base=0, channel_multiplier=0,
                           allow_small_or_imprecise_dtypes=True).then_inc(s_const, 1)
            nc.gpsimd.iota(nar, pattern=[[1, N_STATE]], base=1, channel_multiplier=0,
                           allow_small_or_imprecise_dtypes=True).then_inc(s_const, 1)
            nc.gpsimd.iota(kramp, pattern=[[1, LENGTH]], base=0, channel_multiplier=0,
                           allow_small_or_imprecise_dtypes=True).then_inc(s_const, 1)
            nc.gpsimd.memset(kpad[:, 0:P, :], 0.0).then_inc(s_const, 1)

            link(nc.gpsimd.memset(sel[:, :], 0.0))
            link(nc.gpsimd.affine_select(out=sel[:, :], in_=sel[:, :], compare_op=ALU.not_equal, fill=1.0,
                                         base=0, pattern=[[-1, E]], channel_multiplier=1))
            nc.gpsimd.affine_select(out=sel[:, :], in_=sel[:, :], compare_op=ALU.not_equal, fill=1.0,
                                    base=-32, pattern=[[-1, E]], channel_multiplier=1).then_inc(s_const, 1)
            nc.gpsimd.memset(b1rows[:, :], 0.0).then_inc(s_const, 1)
            nc.gpsimd.memset(b2rows[:, :], 0.0).then_inc(s_const, 1)

            def scatter(layer, g):
                q = lg_of(layer, g)
                pool.wait_ge(s_route, q + 1)
                for t in range(TG):
                    if q == 0 and t == TG // 4:
                        pool.wait_ge(s_wmax, 1)
                        nc.gpsimd.partition_all_reduce(wmax[:, :], wsc[:, 0:2], P, RMAX).then_inc(s_wall, 1)
                    for k in range(TOP_K):
                        i = t * TOP_K + k
                        uses = q * (TG * TOP_K // SC_SEMS) + i // SC_SEMS
                        if uses:
                            pool.wait_ge(s_scat[i % SC_SEMS], 16 * uses)
                        pool.indirect_dma_start(
                            out=slot_x[g],
                            out_offset=bass.IndirectOffsetOnAxis(ap=slots[:, q, k, t:t + 1].bitcast(U32), axis=0),
                            in_=xhl[:, g * TG + t, :, :].rearrange("p s c -> p (s c)"), in_offset=None).then_inc(s_scat[i % SC_SEMS], 16)

            def gather(layer, g):
                q = lg_of(layer, g)
                for u in range(YS_RING):
                    pool.wait_ge(s_yst[u], 16 * len([n for n in range((q + 1) * ST) if n % YS_RING == u]))
                for t in range(TG):
                    n = q * TG + t
                    if n >= YG_RING:
                        pool.wait_ge(s_comb, n - YG_RING + 1)
                    for k in range(TOP_K):
                        pool.indirect_dma_start(
                            out=yg[:, n % YG_RING, k, :], out_offset=None, in_=slot_y[layer][g],
                            in_offset=bass.IndirectOffsetOnAxis(ap=slots[:, q, k, t:t + 1].bitcast(U32), axis=0),
                        ).then_inc(s_yg[k][n % YG_RING], 16)

            pool.wait_ge(s_zfill, 16 * G)
            scatter(0, 0)
            scatter(0, 1)
            gather(0, 0)
            gather(0, 1)
            scatter(1, 0)
            scatter(1, 1)
            gather(1, 0)
            gather(1, 1)

        @block.scalar
        def _(act):
            act.dma_start(ldt, log_dt.rearrange("(d a) -> d a", a=1)).then_inc(s_s4, 16)
            act.dma_start(sbt, s4_b).then_inc(s_s4, 16)
            act.dma_start(sct, s4_c).then_inc(s_s4, 16)
            act.dma_start(dcol, s4_d.rearrange("(d a) -> d a", a=1)).then_inc(s_s4, 16)
            act.wait_ge(s_zero, 1)
            for g in range(G):
                act.dma_start(slot_x[g].rearrange("(t p) c -> p t c", p=P),
                              zero16.rearrange("p (a c) -> p a c", a=1).to_broadcast([P, ST, 2 * D])).then_inc(s_zfill, 16)
            act.wait_ge(s_bzero, 2)
            for row in (0, 32):
                act.dma_start(b1f[row:row + E, :], b1).then_inc(s_b1, 16)
            for row in (0, 32, 64):
                act.dma_start(b2f[row:row + 1, :], b2.rearrange("(a e) c -> a (e c)", a=1)).then_inc(s_b2, 16)

            def high_parts(kind, layer, g):
                def copy(m):
                    act.wait_ge(s_xnt, m + 1)
                    if m >= 2:
                        act.wait_ge(s_gate, m - 1)
                    nc.scalar.activation(xnt[:, m % 2, :], CBK[m % 2][:, 0:P], ACT.Copy).then_inc(s_xntc, 1)

                gate_tile = lg_of(layer, g) * TG
                for i in range(TG):
                    n = norm_base(kind, layer, g) + i
                    act.wait_ge(s_xn, n + 1)
                    nc.scalar.activation(xhl[:, g * TG + i, 0, :], xn[:, n % XN_RING, :], ACT.Copy).then_inc(s_xh, 1)
                    if kind == "router" and i:
                        copy(gate_tile + i - 1)
                if kind == "router":
                    copy(gate_tile + TG - 1)

            def router_exps(layer, g):
                q = lg_of(layer, g)
                act.wait_ge(s_rsub, 2 * q + 1)
                nc.scalar.activation(sc[:, :, :], lg[:, :, :], ACT.Exp).then_inc(s_rexp, 1)
                act.wait_ge(s_rsub, 2 * q + 2)
                nc.scalar.activation(m2[:, :], mt[:, :], ACT.Exp).then_inc(s_rexp, 1)

            def reversed_copies(g):
                for i in range(TG // 2):
                    n = g * (TG // 2) + i
                    act.wait_ge(s_rev, n + 1)
                    nc.scalar.activation(xhl[:, 2 * n:2 * n + 2, :, :].rearrange("p t s c -> p (t s c)"),
                                         CBK[n % 2][:, :], ACT.Copy).then_inc(s_revc, 1)

            def weights_high():
                act.wait_ge(s_kin, 1)
                for e in range(E):
                    dst = w1hl[:, e * 1024:e * 1024 + 512].rearrange("p (k q) -> p k q", k=HC)
                    src = w1st[:, e * HID:(e + 1) * HID].rearrange("p (q k) -> p k q", k=HC)
                    nc.scalar.activation(dst, src, ACT.Copy, scale=wsc[:, 2:3]).then_inc(s_wh, 1)
                w2v = w2hl[:, :].rearrange("p (e s h) -> p e s h", e=E, s=2)
                nc.scalar.activation(w2v[:, :, 0, :], w2st.rearrange("p (e h) -> p e h", e=E), ACT.Copy,
                                     scale=wsc[:, 3:4]).then_inc(s_wh, 1)

            def kernel_power(n, i):
                act.wait_ge(s_kacc, n + 1)
                nc.scalar.activation(kexp[i % KEXP_RING], kramp, ACT.Exp, scale=loga[:, bass.ds(n, 1)]).then_inc(s_kexp, 1)

            def experts(layer, g, kernel=False):
                base = lg_of(layer, g) * ST

                def copy_xt(n, u):
                    act.wait_ge(s_xt, n + 1)
                    if not first(n, 2):
                        act.wait_ge(s_h, n - 1)
                    nc.scalar.activation(xt[:, u % 2, :], XB[u % 2][:, 0:P].bitcast(F16), ACT.Copy).then_inc(s_xtc, 1)

                def relu(n, u):
                    act.wait_ge(s_h, n + 1)
                    if not first(n, 2):
                        act.wait_ge(s_y, n - 1)
                    nc.scalar.activation(hh[:, u % 2, :], HB[u % 2][:, :], ACT.Relu).then_inc(s_relu, 1)

                copy_xt(base, 0)

                def octet(n0, r, start, end):
                    for u in range(OCTET):
                        if not (end and u == OCTET - 1):
                            copy_xt(n0 + u + 1, u + 1)
                        relu(n0 + u, u)
                        if kernel and not start:
                            for i in (2 * u, 2 * u + 1):
                                kernel_power((r - 1) * 2 * OCTET + i, i)
                run_octets(act, base, octet, peel_last=True)

            act.wait_ge(s_s4, 64)
            nc.scalar.activation(dtt, ldt, ACT.Exp).then_inc(s_ac, 1)
            high_parts("router", 0, 0)
            router_exps(0, 0)
            act.wait_ge(s_kt, 1)
            nc.scalar.activation(th, dta, ACT.Tanh, scale=0.5).then_inc(s_ac, 1)
            weights_high()
            high_parts("router", 0, 1)
            router_exps(0, 1)
            act.wait_ge(s_kt, 2)
            experts(0, 0, kernel=True)
            experts(0, 1)
            for g in range(G):
                high_parts("conv", 1, g)
                reversed_copies(g)
                high_parts("router", 1, g)
                router_exps(1, g)
            experts(1, 0)
            experts(1, 1)

        @block.vector
        def _(dve):
            V = nc.vector
            done = [0]

            def link(ins):
                done[0] += 1
                ins.then_inc(s_chain, 1)
                dve.wait_ge(s_chain, done[0])

            norm_n = [0]

            def normalise(tiles, wait_input=None, wait_place=None):
                for i, t in enumerate(tiles):
                    if wait_input:
                        wait_input(t)
                    ins = V.bn_stats(st6[:, i, :], xa[:, t, :])
                link(ins)
                for i, t in enumerate(tiles):
                    ins = V.bn_aggr(mv[:, i, :], st6[:, i, :])
                link(ins)
                mean, var = mv[:, :, 0], mv[:, :, 1]
                link(V.tensor_scalar(nt1[:, :], var, EPS, None, ALU.add))
                link(V.tensor_scalar(nv[:, :], nt1[:, :], -0.5, None, ALU.mult))
                link(V.tensor_scalar(rstd[:, :].bitcast(I32), nt1[:, :].bitcast(I32), -0.5, float(0x5F3759DF), ALU.mult, ALU.add))
                for _ in range(3):
                    link(V.tensor_tensor(nt1[:, :], rstd[:, :], nv[:, :], ALU.mult))
                    link(V.tensor_tensor(nt1[:, :], nt1[:, :], rstd[:, :], ALU.mult))
                    link(V.scalar_tensor_tensor(rstd[:, :], nt1[:, :], 1.5, rstd[:, :], ALU.add, ALU.mult))
                def low(i):
                    n = norm_n[0] - TG + i
                    dve.wait_ge(s_xh, n + 1)
                    V.tensor_tensor(xhl[:, tiles[i], 1, :], xn[:, n % XN_RING, :], xhl[:, tiles[i], 0, :],
                                    ALU.subtract).then_inc(s_xl, 1)

                norm_n[0] += TG
                for i, t in enumerate(tiles):
                    n = norm_n[0] - TG + i
                    if wait_place:
                        wait_place()
                    if n >= XN_RING:
                        dve.wait_ge(s_xl, n - XN_RING + 1)
                    V.tensor_scalar(xn[:, n % XN_RING, :], xa[:, t, :], mv[:, i, 0:1], rstd[:, i:i + 1],
                                    ALU.subtract, ALU.mult).then_inc(s_xn, 1)
                    if i >= 2:
                        low(i - 2)
                low(TG - 2)
                low(TG - 1)

            gate_n = [0]

            def x_loaded(t):
                if t % (NT // 4) == 0:
                    dve.wait_ge(s_x[t // (NT // 4)], 16)

            def xn_place():
                m = gate_n[0]
                gate_n[0] += 1
                if m >= XN_RING:
                    dve.wait_ge(s_xnt, m - XN_RING + 1)

            def bc_e(a):
                return a.rearrange("p (t a) -> p t a", a=1).to_broadcast([P, TG, E])

            def bc_t(a):
                return a.rearrange("p (a e) -> p a e", a=1).to_broadcast([P, TG, E])

            def route(layer, g):
                q = lg_of(layer, g)
                dve.wait_ge(s_gate, (q + 1) * TG)
                ins = V.tensor_tensor(lg[:, :, :], LG[:, 0:TE].rearrange("p (t e) -> p t e", e=E), bc_t(bgs[:, :]), ALU.add)
                ins.then_inc(s_logit, 1)
                dve.wait_ge(s_logit, q + 1)
                link(V.tensor_reduce(m1[:, :], lg[:, :, :], AX.X, ALU.max))
                V.tensor_tensor(lg[:, :, :], lg[:, :, :], bc_e(m1[:, :]), ALU.subtract).then_inc(s_rsub, 1)
                dve.wait_ge(s_rexp, 2 * q + 1)
                link(V.tensor_reduce(m1[:, :], sc[:, :, :], AX.X, ALU.add))
                link(V.reciprocal(m2[:, :], m1[:, :]))
                link(V.tensor_tensor(sc[:, :, :], sc[:, :, :], bc_e(m2[:, :]), ALU.mult))
                for k, m in ((0, m1), (1, m2)):
                    link(V.tensor_reduce(m[:, :], sc[:, :, :], AX.X, ALU.max))
                    link(V.tensor_tensor(eq[:, :, :], sc[:, :, :], bc_e(m[:, :]), ALU.is_equal))
                    link(V.tensor_tensor(eq[:, :, :], eq[:, :, :], bc_t(prio[:, :]), ALU.mult))
                    link(V.tensor_reduce(mt[:, :], eq[:, :, :], AX.X, ALU.max))
                    link(V.tensor_tensor(oh[k][:, :, :], eq[:, :, :], bc_e(mt[:, :]), ALU.is_equal))
                    if k == 0:
                        link(V.scalar_tensor_tensor(sc[:, :, :], oh[0][:, :, :], -2.0, sc[:, :, :], ALU.mult, ALU.add))
                V.tensor_tensor(ohs[:, :, :], oh[0][:, :, :], oh[1][:, :, :], ALU.add).then_inc(s_oh, 1)
                V.tensor_tensor(mt[:, :], m2[:, :], m1[:, :], ALU.subtract).then_inc(s_rsub, 1)
                dve.wait_ge(s_rexp, 2 * q + 2)
                link(V.tensor_scalar(m1[:, :], m2[:, :], 1.0, None, ALU.add))
                link(V.reciprocal(mt[:, :], m1[:, :]))
                link(V.tensor_scalar(prob[:, q, 0, :], mt[:, :], 0.5, None, ALU.mult))
                link(V.tensor_tensor(prob[:, q, 1, :], prob[:, q, 0, :], m2[:, :], ALU.mult))
                dve.wait_ge(s_pre, q + 1)
                link(V.tensor_copy(tot[:, :, :].rearrange("p e t -> p t e"),
                                   CBK[0][:, TE:2 * TE].rearrange("p (t e) -> p t e", e=E)))
                link(V.tensor_tensor_scan(cum[:, :, :].rearrange("p e t -> p (e t)"), segm[:, :, :].rearrange("p e t -> p (e t)"),
                                          tot[:, :, :].rearrange("p e t -> p (e t)"), 0.0, ALU.mult, ALU.add))
                link(V.tensor_scalar(cnti[:, :], cum[:, :, TG - 1], float(P - 1), None, ALU.add))
                link(V.tensor_scalar(cnti[:, :], cnti[:, :], -P, None, ALU.bitwise_and))
                link(V.tensor_copy(cnt[:, :], cnti[:, :]))
                link(V.tensor_tensor_scan(ends[:, :], one8[:, :], cnt[:, :], 0.0, ALU.mult, ALU.add))
                link(V.tensor_tensor(cnt[:, :], ends[:, :], cnt[:, :], ALU.subtract))
                link(V.tensor_tensor(cum[:, :, :], cum[:, :, :], tot[:, :, :], ALU.subtract))
                link(V.tensor_tensor(pos[:, :, :], cum[:, :, :].rearrange("p e t -> p t e"), bc_t(cnt[:, :]), ALU.add))
                link(V.tensor_tensor(pos[:, :, :], CBK[0][:, 0:TE].rearrange("p (t e) -> p t e", e=E), pos[:, :, :], ALU.add))
                for k in range(TOP_K):
                    link(V.tensor_tensor(eq[:, :, :], oh[k][:, :, :], pos[:, :, :], ALU.mult))
                    link(V.tensor_reduce(slotf[:, :], eq[:, :, :], AX.X, ALU.add))
                    link(V.tensor_copy(slots[:, q, k, :], slotf[:, :]))
                dve.wait_ge(s_xl, norm_n[0])
                link(V.tensor_tensor(et1, ends[0:1, :].rearrange("p (a e) -> p a e", a=1).to_broadcast([1, ST, E]),
                                     tstart[:, :, :], ALU.is_le))
                link(V.tensor_reduce(et2[:, :], et1, AX.X, ALU.add))
                V.tensor_scalar(etab[:, q * ST:(q + 1) * ST], et2[:, :], float(E - 1), None, ALU.min).then_inc(s_route, 1)
                dve.wait_ge(s_route, q + 1)

            def weight_scales():
                dve.wait_ge(s_w1, 16)
                link(V.tensor_reduce(wsc[:, 0:1], w1st, AX.X, ALU.max, apply_absolute_value=True))
                dve.wait_ge(s_b1, 32)
                link(V.tensor_reduce(wsc[:, 1:2], b1f, AX.X, ALU.max, apply_absolute_value=True))
                link(V.tensor_tensor(wsc[:, 0:1], wsc[:, 0:1], wsc[:, 1:2], ALU.max))
                dve.wait_ge(s_w2, 16)
                link(V.tensor_reduce(wsc[:, 1:2], w2st, AX.X, ALU.max, apply_absolute_value=True))
                V.tensor_scalar(wsc[:, 0:2], wsc[:, 0:2], TINY, None, ALU.max).then_inc(s_wmax, 1)

            def bias_rows():
                dve.wait_ge(s_wall, 1)
                link(V.tensor_scalar(wsc[:, 2:4].bitcast(I32), wmax[:, 0:2].bitcast(I32), EXPONENT, EXPONENT,
                                     ALU.bitwise_and, ALU.bitwise_xor))
                link(V.tensor_scalar(wsc[:, 4:6].bitcast(I32), wmax[:, 0:2].bitcast(I32), EXPONENT, None, ALU.bitwise_and))
                link(V.tensor_scalar(wsc[:, 4:6], wsc[:, 4:6], 0.5, None, ALU.mult))
                link(V.tensor_tensor(wsc[:, 6:7], wsc[:, 4:5], wsc[:, 5:6], ALU.mult))
                V.tensor_tensor(wsc[:, 7:8], wsc[:, 2:3], wsc[:, 3:4], ALU.mult).then_inc(s_kin, 1)
                dve.wait_ge(s_kin, 1)
                link(V.tensor_scalar(b1f, b1f, wsc[:, 2:3], None, ALU.mult))
                link(V.tensor_copy(b1rows[0:E, :], b1f[0:E, :]))
                link(V.tensor_copy(b1rows[32:32 + E, :], b1f[32:32 + E, :]))
                link(V.tensor_tensor(b1rows[32:32 + E, :], b1f[32:32 + E, :], b1rows[32:32 + E, :], ALU.subtract))
                dve.wait_ge(s_b2, 48)
                link(V.tensor_scalar(b2f, b2f, wsc[:, 7:8], None, ALU.mult))
                for rows in (96, 64, 32):
                    if rows < 96:
                        link(V.tensor_tensor(b2f[0:rows, :], b2f[0:rows, :], b2rows[0:rows, :], ALU.subtract))
                    link(V.tensor_copy(b2rows[0:rows, :], b2f[0:rows, :]))

            def weights_low():
                dve.wait_ge(s_wh, E + 1)
                for e in range(E):
                    o = e * 1024
                    V.scalar_tensor_tensor(
                        w1hl[:, o + 512:o + 1024].rearrange("p (k q) -> p k q", k=HC),
                        w1st[:, e * HID:(e + 1) * HID].rearrange("p (q k) -> p k q", k=HC), wsc[:, 2:3],
                        w1hl[:, o:o + 512].rearrange("p (k q) -> p k q", k=HC), ALU.mult, ALU.subtract)
                w2v = w2hl[:, :].rearrange("p (e s h) -> p e s h", e=E, s=2)
                dve.wait_ge(s_kin, 1)
                V.scalar_tensor_tensor(w2v[:, :, 1, :], w2st.rearrange("p (e h) -> p e h", e=E), wsc[:, 3:4],
                                       w2v[:, :, 0, :], ALU.mult, ALU.subtract).then_inc(s_wready, 1)

            def kernel_arguments():
                dve.wait_ge(s_const, 16)
                dve.wait_ge(s_ac, 1)
                V.tensor_scalar(dta, nar, dtt, -0.5, ALU.mult, ALU.mult).then_inc(s_kt, 1)
                dve.wait_ge(s_kt, 1)
                link(V.tensor_scalar(loga, dta, LOG_FLOOR, None, ALU.max))
                link(V.reciprocal(rn, nar))
                dve.wait_ge(s_ac, 2)
                link(V.tensor_scalar(rden, th, -1.0, 1.0, ALU.mult, ALU.add))
                link(V.reciprocal(kw, rden))
                link(V.scalar_tensor_tensor(rden, th, -4.0, kw, ALU.mult, ALU.mult))
                link(V.tensor_tensor(rden, rden, rn, ALU.mult))
                link(V.tensor_tensor(rden, rden, sbt, ALU.mult))
                V.tensor_tensor(kw, rden, sct, ALU.mult).then_inc(s_kt, 1)
                V.memset(kacc, 0.0).then_inc(s_kacc, KEXP_RING)
                dve.wait_ge(s_kt, 2)

            def kernel_sum(n, i):
                dve.wait_ge(s_kexp, n + 1)
                dve.wait_ge(s_kacc, n + KEXP_RING)
                V.scalar_tensor_tensor(kacc, kexp[i % KEXP_RING], kw[:, bass.ds(n, 1)], kacc,
                                       ALU.mult, ALU.add).then_inc(s_kacc, 1)

            def kernel_rows():
                dve.wait_ge(s_kacc, N_STATE + KEXP_RING)
                link(V.tensor_tensor(kacc[:, 0:1], kacc[:, 0:1], dcol, ALU.add))
                link(V.tensor_reduce(kmx, kacc, AX.X, ALU.max, apply_absolute_value=True))
                link(V.tensor_scalar(kmx, kmx, 1e-30, None, ALU.max))
                link(V.tensor_scalar(kal.bitcast(I32), kmx.bitcast(I32), EXPONENT, EXPONENT, ALU.bitwise_and, ALU.bitwise_xor))
                link(V.tensor_scalar(kiv.bitcast(I32), kmx.bitcast(I32), EXPONENT, None, ALU.bitwise_and))
                link(V.tensor_scalar(kiv, kiv, 0.5, None, ALU.mult))
                V.tensor_scalar(kdiag, ident[:, :], kiv, None, ALU.mult).then_inc(s_kdiag, 1)
                link(V.tensor_scalar(kpad[:, P:, 0], kacc, kal, None, ALU.mult))
                V.scalar_tensor_tensor(kpad[:, P:, 1], kacc, kal, kpad[:, P:, 0], ALU.mult, ALU.subtract).then_inc(s_kpad, 1)
                dve.wait_ge(s_kinv, 1)
                V.tensor_copy(kinv[:, :], CBK[1][:, 0:D]).then_inc(s_kinvc, 1)

            def experts(layer, g, kernel=False, combined=None):
                base = lg_of(layer, g) * ST

                def split(n, u):
                    dve.wait_ge(s_relu, n + 1)
                    V.scalar_tensor_tensor(hl[:, u % 2, :], HB[u % 2][:, :], 0.0, hh[:, u % 2, :],
                                           ALU.max, ALU.subtract).then_inc(s_hl, 1)

                def output(n, u):
                    dve.wait_ge(s_y, n + 1)
                    if not first(n, YS_RING):
                        dve.wait_ge(s_yst[u % YS_RING], (n - u % YS_RING) * (16 // YS_RING))
                    V.tensor_copy(ysb[:, u % YS_RING, :], YB[u % 2][:, 0:D]).then_inc(s_yc, 1)

                def octet(n0, r, start, end):
                    for u in range(OCTET):
                        split(n0 + u, u)
                        if not start or u >= 2:
                            output(n0 + u - 2, u - 2)
                        if kernel and not start:
                            for i in (2 * u, 2 * u + 1):
                                kernel_sum((r - 1) * 2 * OCTET + i, i)
                        if combined and not start and u % 2:
                            combine_tile(*combined, (r - 1) * YG_RING + u // 2, u // 2)
                run_octets(dve, base, octet)
                for u in (OCTET - 2, OCTET - 1):
                    output(base + ST - OCTET + u, u)
                if combined:
                    dve.wait_ge(s_comb, (lg_of(*combined) + 1) * TG)

            def combine_tile(layer, g, t, r):
                q = lg_of(layer, g)
                n = t + q * TG
                tile = xa[:, bass.ds(t + g * TG, 1), :].rearrange("p a c -> p (a c)")
                for k in range(TOP_K):
                    dve.wait_ge(s_yg[k][r], (n - r) * (16 // YG_RING) + 16)
                p = [prob[:, q, k, bass.ds(t, 1)] for k in range(TOP_K)]
                V.scalar_tensor_tensor(tile, yg[:, r, 0, :], p[0], tile, ALU.mult, ALU.add).then_inc(s_part, 1)
                dve.wait_ge(s_part, n + 1)
                V.scalar_tensor_tensor(tile, yg[:, r, 1, :], p[1], tile, ALU.mult, ALU.add).then_inc(s_comb, 1)

            def combine(layer, g, tiles=range(TG)):
                for t in tiles:
                    combine_tile(layer, g, t, t % YG_RING)
                dve.wait_ge(s_comb, lg_of(layer, g) * TG + tiles[-1] + 1)

            def scale_prob(q0, q1):
                v = prob[:, q0:q1, :, :].rearrange("p q k t -> p (q k t)")
                link(V.tensor_scalar(v, v, wsc[:, 6:7], None, ALU.mult))

            def conv_input(g):
                for k in range(SC_SEMS):
                    dve.wait_ge(s_scat[k], 16 * G * (TG * TOP_K // SC_SEMS))
                normalise(range(g * TG, (g + 1) * TG))

            cv_n = [0]
            cvt = hsplit[:, :, :].rearrange("p a b -> p (a b)").bitcast(F32)

            def conv_output(g):
                for cb in conv_blocks(g):
                    n = cv_n[0]
                    cv_n[0] += 1
                    dve.wait_ge(s_cv, n + 1)
                    tmp = cvt[:, (n % 2) * 512:(n % 2) * 512 + 512].rearrange("p (t c) -> p t c", c=CB)
                    scale = kinv[:, cb * CB:(cb + 1) * CB].rearrange("p (a c) -> p a c", a=1).to_broadcast([P, TG, CB])
                    V.tensor_tensor(tmp, CBK[n % 2][:, :].rearrange("p (t c) -> p t c", c=CB), scale, ALU.mult).then_inc(s_cve, 1)
                    dve.wait_ge(s_cve, n + 1)
                    dst = xa[:, g * TG:(g + 1) * TG, cb * CB:(cb + 1) * CB]
                    link(V.tensor_tensor(dst, dst, tmp, ALU.add))

            normalise(range(0, TG), x_loaded, xn_place)
            dve.wait_ge(s_wg, 32)
            route(0, 0)
            weight_scales()
            kernel_arguments()
            bias_rows()
            normalise(range(TG, NT), x_loaded, xn_place)
            weights_low()
            route(0, 1)
            scale_prob(0, 2)
            experts(0, 0, kernel=True)
            kernel_rows()
            experts(0, 1, combined=(0, 0))
            conv_input(0)
            combine(0, 1, range(0, TG // 2))
            conv_output(0)
            normalise(range(0, TG), None, xn_place)
            combine(0, 1, range(TG // 2, TG))
            route(1, 0)
            conv_input(1)
            conv_output(1)
            normalise(range(TG, NT), None, xn_place)
            route(1, 1)
            scale_prob(2, 4)
            experts(1, 0)
            experts(1, 1, combined=(1, 0))
            combine(1, 1)

        @block.tensor
        def _(pe):
            b1v = b1rows[:, :].rearrange("p (q k) -> p k q", k=HC)

            def mm(o, a, b, start, stop):
                return nc.tensor.matmul(o, lhsT=a, rhs=b, start=start, stop=stop)

            def gate(layer, g):
                q = lg_of(layer, g)

                def product(n):
                    t = n - q * TG
                    pe.wait_ge(s_xntc, n + 1)
                    mm(LG[:, t * E:(t + 1) * E], xnt[:, n % 2, :], wgs[:, :], True, True).then_inc(s_gate, 1)

                if q:
                    pe.wait_ge(s_route, q)
                if layer:
                    pe.wait_ge(s_cve, (g + 1) * (D // CB))
                for t in range(TG):
                    n = q * TG + t
                    m = norm_base("router", layer, g) + t
                    pe.wait_ge(s_xn, m + 1)
                    if n >= 2:
                        pe.wait_ge(s_xntc, n - 1)
                    nc.tensor.transpose(CBK[n % 2][:, 0:P], xn[:, m % XN_RING, :], ident[:, :]).then_inc(s_xnt, 1)
                    if t:
                        product(n - 1)
                product(q * TG + TG - 1)
                pe.wait_ge(s_oh, q + 1)
                ohf = ohs[:, :, :].rearrange("p t e -> p (t e)")
                mm(CBK[0][:, 0:TE], before16[:, :], ohf, True, True)
                mm(CBK[0][:, TE:2 * TE], ones16[:, :], ohf, True, True).then_inc(s_pre, 1)

            er = [pe.alloc_register(f"expert{i}") for i in range(4)]
            ep = [pe.alloc_register(f"expert_before{i}") for i in range(2)]

            def experts(layer, g):
                base = lg_of(layer, g) * ST
                pe.wait_ge(s_route, lg_of(layer, g) + 1)

                def front(n, u):
                    pe.wait_ge(s_xs[u % XS_RING], (n - u % XS_RING) * (16 // XS_RING) + 16)
                    if not first(n, 2):
                        pe.wait_ge(s_xtc, n - 1)
                    b = XB[u % 2][:, 0:P].bitcast(F16)
                    nc.tensor.transpose(b[:, 0:P], xs[:, u % XS_RING, 0:P], ident16[:, :])
                    nc.tensor.transpose(b[:, P:2 * P], xs[:, u % XS_RING, P:2 * P], ident16[:, :]).then_inc(s_xt, 1)

                def hidden(n, u, e):
                    pe.wait_ge(s_xtc, n + 1)
                    if not first(n, 2):
                        pe.wait_ge(s_hl, n - 1)
                    xh, xl = xt[:, u % 2, 0:P], xt[:, u % 2, P:2 * P]
                    row = sel[:, bass.ds(e, 1)].to_broadcast([P, P])
                    for k in range(HC):
                        o = HB[u % 2][:, k * P:(k + 1) * P]
                        wh = w1hl[:, bass.ds(e * 1024 + k * P, P)]
                        wl = w1hl[:, bass.ds(e * 1024 + 512 + k * P, P)]
                        mm(o, b1v[:, k, :], row, True, False)
                        mm(o, wh, xh, False, False)
                        mm(o, wh, xl, False, False)
                        last = mm(o, wl, xh, False, True)
                    last.then_inc(s_h, 1)

                def output(n, u, e):
                    pe.wait_ge(s_hl, n + 1)
                    if not first(n, 2):
                        pe.wait_ge(s_yc, n - 1)
                    o = YB[u % 2][:, 0:D]
                    mm(o, ones16[:, :], b2rows[:, bass.ds(e * D, D)], True, False)
                    for k in range(HC):
                        ah, al = hh[:, u % 2, k * P:(k + 1) * P], hl[:, u % 2, k * P:(k + 1) * P]
                        wh = w2hl[:, bass.ds(e * 1024 + k * P, P)]
                        wl = w2hl[:, bass.ds(e * 1024 + 512 + k * P, P)]
                        mm(o, ah, wh, False, False)
                        mm(o, ah, wl, False, False)
                        last = mm(o, al, wh, False, k == HC - 1)
                    last.then_inc(s_y, 1)

                def value(reg):
                    return pe.snap(reg, min_val=0, max_val=E - 1)

                front(base, 0)

                def octet(n0, r, start, end):
                    for half in (0, 4):
                        if half or not start:
                            for i in range(2):
                                pe.reg_mov(ep[i], er[2 + i])
                        pe.load(er, etab[0:1, bass.ds(n0 + half, 4)])
                        for u in range(half, half + 4):
                            if not (end and u == OCTET - 1):
                                front(n0 + u + 1, u + 1)
                            hidden(n0 + u, u, value(er[u - half]))
                            if not start or u >= 2:
                                output(n0 + u - 2, u - 2, value(er[u - half - 2] if u - half >= 2 else ep[u - half]))
                run_octets(pe, base, octet, peel_last=True)
                for i in (2, 3):
                    output(base + ST - 4 + i, i, value(er[i]))

            def reverse(g):
                if g:
                    pe.wait_ge(s_route, LAYERS * G - G + g)
                for i in range(TG // 2):
                    n = g * (TG // 2) + i
                    t = 2 * n
                    pe.wait_ge(s_xl, norm_base("conv", 1, g) + 2 * i + 2)
                    if n >= 2:
                        pe.wait_ge(s_revc, n - 1)
                    mm(CBK[n % 2][:, :], back16[:, :], xhl[:, t:t + 2, :, :].rearrange("p t s c -> p (t s c)"),
                       True, True).then_inc(s_rev, 1)
                pe.wait_ge(s_revc, (g + 1) * (TG // 2))

            def conv(g):
                for i, cb in enumerate(conv_blocks(g)):
                    n = g * (D // CB) + i
                    if i >= 2:
                        pe.wait_ge(s_cve, n - 1)
                    b = CBK[n % 2][:, :].rearrange("p (t c) -> p t c", c=CB)
                    for c in range(CB):
                        d = cb * CB + c
                        part = d // TC
                        if d == 0 and g == 0:
                            pe.wait_ge(s_toep, 16 * T_PLACES * TC // 4)
                        if d == D - TC and g == 0:
                            pe.wait_ge(s_tlast, 16)
                        if d == 0 and g:
                            pe.wait_ge(s_tagain, 16)
                        at = toeplitz_place(part, g) * TC + d % TC
                        th0, tl0 = toep[:, at, 0:2 * P:2], toep[:, at, 1:2 * P:2]
                        th1, tl1 = toep[:, at, 2 * P::2], toep[:, at, 2 * P + 1::2]
                        a, z = g * TG, (g + 1) * TG
                        xh, xl = xhl[:, a:z, 0, d], xhl[:, a:z, 1, d]
                        xh0, xl0 = xhl[:, a:z:2, 0, d], xhl[:, a:z:2, 1, d]
                        o, o1 = b[:, :, c], b[:, 1::2, c]
                        mm(o, th0, xh, True, False)
                        mm(o, th0, xl, False, False)
                        mm(o1, th1, xh0, False, False)
                        mm(o1, th1, xl0, False, False)
                        mm(o1, tl1, xh0, False, False)
                        last = mm(o, tl0, xh, False, True)
                    last.then_inc(s_cv, 1)

            pe.wait_ge(s_const, 16)
            pe.wait_ge(s_wg, 32)
            gate(0, 0)
            gate(0, 1)
            pe.wait_ge(s_wready, 1)
            experts(0, 0)
            pe.wait_ge(s_kdiag, 1)
            mm(CBK[1][:, 0:D], onesf, kdiag, True, True).then_inc(s_kinv, 1)
            experts(0, 1)
            pe.wait_ge(s_kinvc, 1)
            for g in range(G):
                reverse(g)
                conv(g)
                gate(1, g)
            experts(1, 0)
            experts(1, 1)


_INS = ['L0_attn_x', 'L0_attn_log_dt', 'L0_attn_B', 'L0_attn_C', 'L0_attn_D', 'L0_ffn_W1', 'L0_ffn_b1',
        'L0_ffn_W2', 'L0_ffn_b2', 'L0_ffn_Wg', 'L0_ffn_bg']


def kernel(**inputs):
    import numpy as _np
    import concourse.bacc as _bacc
    from concourse import mybir as _mybir
    from concourse.bass_utils import run_bass_kernel_spmd as _run

    nc = _bacc.Bacc("TRN2", target_bir_lowering=False, num_devices=1)
    arrays, args = {}, []
    for name in _INS:
        a = _np.ascontiguousarray(inputs[name])
        arrays[f"in_{name}_dram"] = a
        args.append(nc.dram_tensor(f"in_{name}_dram", a.shape, _mybir.dt.from_np(a.dtype), kind="ExternalInput").ap())
    args.append(nc.dram_tensor("out_0_dram", (BATCH, LENGTH, D), _mybir.dt.float32, kind="ExternalOutput").ap())
    macaron_kernel(nc, *args)
    r = _run(nc, [arrays], core_ids=[0])
    return r.results[0]["out_0_dram"]
```

```python
import concourse.bass as bass
from concourse import mybir
from contextlib import ExitStack

P = 128
BATCH, LENGTH, D = 16, 256, 128
N_STATE = 64
E, HID, TOP_K = 8, 512, 2
HC = HID // P
NT = BATCH * LENGTH // P
G = 2
TG = NT // G
BR = 2 * P
ROUND = 4
NB = (TG * P * TOP_K - E) // BR + E
ROW = 2 * D + 2
SPARE = NB * BR
ROUNDS = -(-NB // ROUND)
STATES_PER_BLOCK = N_STATE // ((ROUNDS - 2) * ROUND)
LAYERS = 2
EPS = 1e-5
LOG_FLOOR = -23.025850929940457
XS_RING, YS_RING, XN_RING, YG_RING, XNT_RING = 4, 4, 4, 4, 3
TINY = 1e-15
SC_SEMS = 8
EXPONENT = 0x7F800000
KPAD = LENGTH + P
CB = 32
TC = 16
T_PARTS = D // TC
T_PLACES = T_PARTS - 1


def toeplitz_place(part, g):
    return part if part not in (0, T_PARTS - 1) else (0 if part else (0 if g == 0 else 2))


def conv_blocks(g):
    return [0, 1, 2, 3] if g == 0 else [1, 2, 3, 0]


def run_rounds(eng, base, blocks, straight=False):
    if straight:
        for r in range(ROUNDS):
            blocks(base + r * ROUND, r, r == 0, r == ROUNDS - 1)
        return
    blocks(base, 0, True, False)
    with eng.Fori(1, ROUNDS - 1) as r:
        blocks(r * ROUND + base, r, False, False)
    blocks(base + (ROUNDS - 1) * ROUND, ROUNDS - 1, False, True)


def block_steps(base, end):
    return [(u, base + u) for u in range(NB - (ROUNDS - 1) * ROUND if end else ROUND)]


NORMS = {("router", 0, 0): TG, ("router", 0, 1): TG, ("conv_a", 1, 1): TG // 2, ("conv_b", 1, 1): TG // 2,
         ("router", 1, 0): TG, ("router", 1, 1): TG}
HALVES = {"conv_a": range(TG // 2), "conv_b": range(TG // 2, TG), "router": range(TG)}


def norm_base(kind, layer, g):
    keys = list(NORMS)
    return sum(NORMS[k] for k in keys[:keys.index((kind, layer, g))])


def output_ring(g):
    return YG_RING + XS_RING if g == G - 1 else YG_RING


def first(n, count):
    return isinstance(n, int) and n < count


def macaron_kernel(nc, x, log_dt, s4_b, s4_c, s4_d, w1, b1, w2, b2, wg, bg, out):
    F32, F16, BF16, I32, U32 = mybir.dt.float32, mybir.dt.float16, mybir.dt.bfloat16, mybir.dt.int32, mybir.dt.uint32
    ALU, ACT, AX = mybir.AluOpType, mybir.ActivationFunctionType, mybir.AxisListType
    RMAX = bass.bass_isa.ReduceOp.max

    with ExitStack() as ctx:
        def sb(name, shape, dt=F32):
            return ctx.enter_context(nc.sbuf_tensor(name, shape, dt))

        def sem(name):
            return ctx.enter_context(nc.semaphore(name))

        def sems(name, n):
            return [sem(f"{name}{i}") for i in range(n)]

        slot_x = [nc.dram_tensor(f"slot_x{g}", [NB * BR, ROW], F16, kind="Internal").ap() for g in range(G)]
        pair_y = [[nc.dram_tensor(f"pair_y{l}{g}", [SPARE + TOP_K * TG * P, D], F32, kind="Internal").ap()
                   for g in range(G)] for l in range(LAYERS)]
        kern_d = nc.dram_tensor("kern_d", [P, 2 * KPAD], F16, kind="Internal").ap()

        xa = sb("xa", [P, NT, D])
        xrow = sb("xrow", [P, NT, ROW], F16)
        xparts = xrow[:, :, 0:2 * D]
        xhl = xparts.rearrange("p t (s c) -> p t s c", s=2)
        w1p = [[sb(f"w1p{s}{k}", [P, E * P], F16) for k in range(HC)] for s in range(2)]
        w2p = [sb(f"w2p{k}", [P, E * 2 * D], F16) for k in range(HC)]
        toep = sb("toep", [P, T_PLACES * TC, 2 * LENGTH], F16)
        b1rows = sb("b1rows", [P, P], F16)
        b2rows = sb("b2rows", [P, D], BF16)
        sel = sb("sel", [P, E * HC], F16)
        sel3 = sb("sel3", [P, E], F16)
        wgs = sb("wgs", [P, E])
        bgs = sb("bgs", [P, E])
        ident = sb("ident", [P, P])
        ident16 = sb("ident16", [P, P], F16)
        before16 = sb("before16", [P, P], F16)
        ones16 = sb("ones16", [P, P], F16)
        back16 = sb("back16", [P, P], F16)
        kinv = sb("kinv", [P, D])
        wsc = sb("wsc", [P, 8])
        wmax = sb("wmax", [P, 2])
        xs = sb("xs", [P, XS_RING, 2, ROW], F16)
        xt = sb("xt", [P, 2, 2 * BR], F16)
        hsplit = sb("hsplit", [P, 4, HC * BR], F16)
        hh, hl = hsplit[:, 0:2, :], hsplit[:, 2:4, :]
        ysb = sb("ysb", [P, YS_RING, 2, D])
        yg = sb("yg", [P, YG_RING, TOP_K, D])
        rowid = sb("rowid", [P, YS_RING, 2], I32)
        ids = sb("ids", [P, TOP_K, TG], I32)
        spare = sb("spare", [P, 2 * NB, 1], I32)
        between = hsplit[:, :, :].rearrange("p a b -> p (a b)").bitcast(F32)
        cvt = between[:, 0:1024].rearrange("p (a b) -> p a b", a=2)
        xn = between[:, 1024:1024 + XN_RING * D].rearrange("p (a c) -> p a c", a=XN_RING)
        xnt = between[:, 1536:1536 + XNT_RING * P].rearrange("p (a c) -> p a c", a=XNT_RING)
        TE = TG * E
        mv = sb("mv", [P, NT, 2])
        st6 = sb("st6", [P, TG, 6])
        rstd = sb("rstd", [P, TG])
        nmr = sb("nmr", [P, TG])
        xm = sb("xm", [P, 2, D])
        lg = sb("lg", [P, TG, E])
        sc = sb("sc", [P, TG, E])
        eq = sb("eq", [P, TG, E])
        oh = sb("oh", [P, TOP_K, TE], F16)
        ohk = [oh[:, k, :].rearrange("p (t e) -> p t e", e=E) for k in range(TOP_K)]
        chosen = xm[:, :, :]
        slotf = sb("slotf", [P, TOP_K, TG])
        ohs = sb("ohs", [P, TG, E], F16)
        m1 = sb("m1", [P, TG])
        m2 = sb("m2", [P, TG])
        mt = sb("mt", [P, TG])
        nv, nt1 = m1, mt
        cum = between[:, 1920:1920 + TE].rearrange("p (e t) -> p e t", e=E)
        pos = between[:, 1792:1792 + TE].rearrange("p (t e) -> p t e", e=E)
        cnt = sb("cnt", [P, E])
        cnti = sb("cnti", [P, E], I32)
        ends = sb("ends", [P, E])
        slots = sb("slots", [P, LAYERS * G, TOP_K, TG], I32)
        prob = sb("prob", [P, LAYERS * G, TOP_K, TG])
        et1 = between[0:1, 1024:1024 + NB * E].rearrange("p (j e) -> p j e", e=E)
        et2 = sb("et2", [1, NB])
        etab = sb("etab", [1, LAYERS * G * NB], I32)
        prio = sb("prio", [P, E])
        segm = sb("segm", [P, E, TG], F16)
        one8 = sb("one8", [P, E])
        tstart = sb("tstart", [1, NB, E], F16)
        yplace = [yg[:, r, :, :] for r in range(YG_RING)] + \
                 [xs[:, r, :, :].rearrange("p a c -> p (a c)")[:, 0:2 * TOP_K * D].bitcast(F32).rearrange("p (k c) -> p k c", k=TOP_K)
                  for r in range(XS_RING)]
        zero16 = xt[:, 0, 0:2 * D]
        tview = toep[:, :, :].rearrange("p a b -> p (a b)").bitcast(F32)
        used = [0]

        def scratch(n):
            used[0] += n
            assert used[0] <= T_PLACES * TC * LENGTH
            return tview[:, used[0] - n:used[0]]

        w1st, w2st = scratch(E * HID), scratch(E * HID)
        w1chunk = lambda k: w1st.rearrange("p (e k q) -> p e k q", e=E, k=HC)[:, :, k, :]
        w2chunk = lambda k: w2st.rearrange("p (e k c) -> p e k c", e=E, k=HC)[:, :, k, :]
        w1part = lambda s, k: w1p[s][k].rearrange("p (e q) -> p e q", e=E)
        w2part = lambda s, k: w2p[k].rearrange("p (e s c) -> p e s c", e=E, s=2)[:, :, s, :]
        kramp = scratch(LENGTH)
        kexp = scratch(N_STATE * LENGTH).rearrange("p (n l) -> p n l", n=N_STATE)
        ksums = scratch(STATES_PER_BLOCK * LENGTH).rearrange("p (i l) -> p i l", i=STATES_PER_BLOCK)
        kacc = scratch(LENGTH)
        kpad = scratch(KPAD).bitcast(F16).rearrange("p (k s) -> p k s", s=2)
        nar, dta, loga, th, rden, rn, kw, sbt, sct = (scratch(N_STATE) for _ in range(9))
        ldt, dtt, kmx, kal, kiv = (scratch(1) for _ in range(5))
        kdiag = scratch(P)
        onesf = scratch(P)
        dcol = scratch(1)
        wparts = scratch(5)
        b1f, b2f = scratch(P), scratch(D)

        bank = [ctx.enter_context(nc.psum_tensor(f"bank{i}", [P, 512], F32)) for i in range(8)]
        HB, XB, YB = bank[0:4], bank[4:6], bank[6:8]
        CVB, CBK = HB, YB
        LG = XB[0]
        TB = [*CBK, XB[1]]

        s_x = sems("s_x", 4)
        s_w1, s_w2, s_b1, s_b2, s_wg, s_s4 = (sem(n) for n in ("s_w1", "s_w2", "s_b1", "s_b2", "s_wg", "s_s4"))
        s_bzero = sem("s_bzero")
        s_zero = sem("s_zero")
        s_zfill = sem("s_zfill")
        s_const = sem("s_const")
        s_id = sem("s_id")
        s_chain = sem("s_chain")
        s_ac = sem("s_ac")
        s_wmax = sem("s_wmax")
        s_wall = sem("s_wall")
        s_wh = sem("s_wh")
        s_wready = sem("s_wready")
        s_kin = sem("s_kin")
        s_kt = sem("s_kt")
        s_kexp = sem("s_kexp")
        s_kacc = sem("s_kacc")
        s_kpad = sem("s_kpad")
        s_kst = sem("s_kst")
        s_kdiag = sem("s_kdiag")
        s_kinv = sem("s_kinv")
        s_kinvc = sem("s_kinvc")
        s_toep = sem("s_toep")
        s_tlast = sem("s_tlast")
        s_tagain = sem("s_tagain")
        s_stat = sem("s_stat")
        s_xn = sem("s_xn")
        s_xm = sem("s_xm")
        s_xl = sem("s_xl")
        s_xnt = sem("s_xnt")
        s_xntc = sem("s_xntc")
        s_gate = sem("s_gate")
        s_logit = sem("s_logit")
        s_rsub = sem("s_rsub")
        s_rexp = sem("s_rexp")
        s_oh = sem("s_oh")
        s_pre = sem("s_pre")
        s_route = sem("s_route")
        s_scat = sems("s_scat", SC_SEMS)
        s_xs = sems("s_xs", XS_RING)
        s_xt = sem("s_xt")
        s_xtc = sem("s_xtc")
        s_h = sem("s_h")
        s_relu = sem("s_relu")
        s_hl = sem("s_hl")
        s_y = sem("s_y")
        s_rowid = sem("s_rowid")
        s_ya = sem("s_ya")
        s_yc = sem("s_yc")
        s_yst = [sems(f"s_yst{a}", YS_RING) for a in range(2)]
        s_yg = [sems(f"s_yg{g}_", output_ring(g)) for g in range(G)]
        s_part = sem("s_part")
        s_comb = sem("s_comb")
        s_rev = sem("s_rev")
        s_revc = sem("s_revc")
        s_cv = sem("s_cv")
        s_cve = sem("s_cve")
        s_out = sem("s_out")

        x_t = x.rearrange("b (h p) c -> p (b h) c", p=P)
        out_t = out.rearrange("b (h p) c -> p (b h) c", p=P)
        lg_of = lambda layer, g: layer * G + g

        def outputs_of_tile(eng, layer, g, t):
            q = lg_of(layer, g)
            if t == 0:
                for a in range(2):
                    for r in range(YS_RING):
                        eng.wait_ge(s_yst[a][r], 16 * len([n for n in range((q + 1) * NB) if n % YS_RING == r]))
            ring = output_ring(g)
            before = q * TG + max(t - ring + 1, 0)
            if before:
                eng.wait_ge(s_comb, before)
            rows = pair_y[layer][g][SPARE:, :].rearrange("(k t p) c -> p t k c", k=TOP_K, p=P)[:, t, :, :]
            eng.dma_start(yplace[t % ring], rows).then_inc(s_yg[g][t % ring], 16)

        block = ctx.enter_context(nc.Block())

        @block.sync
        def _(sp):
            XQ = NT // 4
            sp.dma_start(xa[:, 0:XQ, :], x_t[:, 0:XQ, :]).then_inc(s_x[0], 16)
            sp.dma_start(xa[:, XQ:2 * XQ, :], x_t[:, XQ:2 * XQ, :]).then_inc(s_x[1], 16)
            sp.dma_start(wgs[:, :], wg).then_inc(s_wg, 16)
            sp.dma_start(bgs[:, :], bg.rearrange("(a e) -> a e", a=1).to_broadcast([P, E])).then_inc(s_wg, 16)
            sp.dma_start(xa[:, 2 * XQ:3 * XQ, :], x_t[:, 2 * XQ:3 * XQ, :]).then_inc(s_x[2], 16)
            sp.dma_start(xa[:, 3 * XQ:, :], x_t[:, 3 * XQ:, :]).then_inc(s_x[3], 16)
            sp.dma_start(w1st.rearrange("p (e h) -> p e h", e=E), w1.rearrange("e c h -> c e h")).then_inc(s_w1, 16)
            sp.dma_start(w2st.rearrange("p (j c) -> p j c", c=D),
                         w2.rearrange("e (k p) c -> p (e k) c", k=HC)).then_inc(s_w2, 16)

            def load_toeplitz(channel, count, place, signal):
                src = bass.AP(kern_d.tensor, 2, [[2, P], [2 * KPAD, P], [1, 2 * LENGTH]])
                sp.dma_start(toep[:, bass.ds(place, count), :], src[:, bass.ds(channel, count), :]).then_inc(signal, 16)

            TD = T_PLACES * TC // ((ROUNDS - 2) * ROUND)

            def expert_io(layer, g, toeplitz=False):
                base = lg_of(layer, g) * NB
                for k in range(SC_SEMS):
                    sp.wait_ge(s_scat[k], 16 * (lg_of(layer, g) + 1) * (TG * TOP_K // SC_SEMS))

                def load(n, v):
                    if not first(n, XS_RING):
                        sp.wait_ge(s_xt, n - (XS_RING - 1))
                        sp.wait_ge(s_rowid, n - (XS_RING - 1))
                    rows = slot_x[g][bass.ds((n - base) * BR, BR), :].rearrange("(a p) c -> p a c", p=P)
                    sp.dma_start(xs[:, v % XS_RING, :, :], rows).then_inc(s_xs[v % XS_RING], 16)

                def blocks(n0, r, start, end):
                    for u, v in block_steps(base, end):
                        load(n0 + u, v)
                        if toeplitz and start and u == 2:
                            sp.wait_ge(s_kpad, 1)
                            sp.dma_start(kern_d, kpad.rearrange("p k s -> p (k s)")).then_inc(s_kst, 16)
                        if toeplitz and start and u == ROUND - 1:
                            sp.wait_ge(s_kst, 16)
                            sp.wait_ge(s_kinvc, 1)
                        if toeplitz and not start and not end:
                            c = (r - 1) * (ROUND * TD) + u * TD
                            load_toeplitz(c, TD, c, s_toep)
                run_rounds(sp, base, blocks)

            def load_outputs(layer, tiles):
                for t in tiles:
                    outputs_of_tile(sp, layer, G - 1, t)

            expert_io(0, 0)
            expert_io(0, 1, toeplitz=True)
            sp.wait_ge(s_zero, 2)
            sp.wait_ge(s_xt, G * NB)
            for g in range(G):
                sp.dma_start(slot_x[g].rearrange("(t p) c -> p t c", p=P)[:, :, 2 * D:], spare[:, :, :].bitcast(F16)).then_inc(s_zfill, 16)
            load_outputs(0, range(TG // 2))
            sp.wait_ge(s_cv, 1)
            load_toeplitz(D - TC, TC, 0, s_tlast)
            load_outputs(0, range(TG // 2, TG))
            sp.wait_ge(s_cv, D // CB + 1)
            load_toeplitz(0, TC, 2 * TC, s_tagain)
            for g in range(G):
                expert_io(1, g)
            for t in range(0, TG, 2):
                sp.wait_ge(s_comb, NT + t + 2)
                sp.dma_start(out_t[:, t:t + 2, :], xa[:, t:t + 2, :]).then_inc(s_out, 16)
            sp.wait_ge(s_xt, LAYERS * G * NB)
            ring = output_ring(G - 1)
            load_outputs(1, range(ring))
            for t in range(TG, NT, 2):
                sp.wait_ge(s_comb, NT + t + 2)
                if t + ring < NT:
                    load_outputs(1, range(t - TG + ring, t - TG + ring + 2))
                sp.dma_start(out_t[:, t:t + 2, :], xa[:, t:t + 2, :]).then_inc(s_out, 16)
            sp.wait_ge(s_out, 16 * NT // 2)

        @block.gpsimd
        def _(pool):
            done = [0]

            def link(ins):
                done[0] += 1
                ins.then_inc(s_id, 1)
                pool.wait_ge(s_id, done[0])

            nc.gpsimd.memset(zero16, 0.0).then_inc(s_zero, 1)
            nc.gpsimd.iota(spare[:, :, :], pattern=[[P, 2 * NB], [0, 1]], base=0, channel_multiplier=1).then_inc(s_zero, 1)
            nc.gpsimd.memset(b1f, 0.0).then_inc(s_bzero, 1)
            nc.gpsimd.memset(b2f, 0.0).then_inc(s_bzero, 1)
            link(nc.gpsimd.memset(ident[:, :], 0.0))
            nc.gpsimd.affine_select(out=ident[:, :], in_=ident[:, :], compare_op=ALU.not_equal, fill=1.0,
                                    base=0, pattern=[[-1, P]], channel_multiplier=1).then_inc(s_const, 1)
            link(nc.gpsimd.memset(ident16[:, :], 0.0))
            nc.gpsimd.affine_select(out=ident16[:, :], in_=ident16[:, :], compare_op=ALU.not_equal, fill=1.0,
                                    base=0, pattern=[[-1, P]], channel_multiplier=1).then_inc(s_const, 1)
            link(nc.gpsimd.memset(back16[:, :], 0.0))
            nc.gpsimd.affine_select(out=back16[:, :], in_=back16[:, :], compare_op=ALU.not_equal, fill=1.0,
                                    base=1 - P, pattern=[[1, P]], channel_multiplier=1).then_inc(s_const, 1)
            nc.gpsimd.iota(ids[:, :, :], pattern=[[TG * P, TOP_K], [P, TG]], base=SPARE, channel_multiplier=1).then_inc(s_zero, 1)
            nc.gpsimd.memset(ones16[:, :], 1.0).then_inc(s_const, 1)
            nc.gpsimd.memset(onesf, 1.0).then_inc(s_const, 1)
            nc.gpsimd.memset(one8[:, :], 1.0).then_inc(s_const, 1)
            link(nc.gpsimd.memset(before16[:, :], 1.0))
            nc.gpsimd.affine_select(out=before16[:, :], in_=before16[:, :], compare_op=ALU.is_gt, fill=0.0,
                                    base=0, pattern=[[1, P]], channel_multiplier=-1).then_inc(s_const, 1)
            link(nc.gpsimd.memset(segm[:, :, :], 1.0))
            nc.gpsimd.memset(segm[:, :, 0:1], 0.0).then_inc(s_const, 1)
            nc.gpsimd.iota(prio[:, :], pattern=[[-1, E]], base=E, channel_multiplier=0,
                           allow_small_or_imprecise_dtypes=True).then_inc(s_const, 1)
            nc.gpsimd.iota(tstart[:, :, :], pattern=[[BR, NB], [0, E]], base=0, channel_multiplier=0,
                           allow_small_or_imprecise_dtypes=True).then_inc(s_const, 1)
            nc.gpsimd.iota(nar, pattern=[[1, N_STATE]], base=1, channel_multiplier=0,
                           allow_small_or_imprecise_dtypes=True).then_inc(s_const, 1)
            nc.gpsimd.iota(kramp, pattern=[[1, LENGTH]], base=0, channel_multiplier=0,
                           allow_small_or_imprecise_dtypes=True).then_inc(s_const, 1)
            nc.gpsimd.memset(kpad[:, 0:P, :], 0.0).then_inc(s_const, 1)

            link(nc.gpsimd.memset(sel[:, :], 0.0))
            link(nc.gpsimd.affine_select(out=sel[:, :], in_=sel[:, :], compare_op=ALU.not_equal, fill=1.0,
                                         base=0, pattern=[[-1, E * HC]], channel_multiplier=1))
            nc.gpsimd.affine_select(out=sel[:, :], in_=sel[:, :], compare_op=ALU.not_equal, fill=1.0,
                                    base=-32, pattern=[[-1, E * HC]], channel_multiplier=1).then_inc(s_const, 1)
            link(nc.gpsimd.memset(sel3[:, :], 0.0))
            for row in (0, 32, 64):
                ins = nc.gpsimd.affine_select(out=sel3[:, :], in_=sel3[:, :], compare_op=ALU.not_equal, fill=1.0,
                                              base=-row, pattern=[[-1, E]], channel_multiplier=1)
                if row < 64:
                    link(ins)
            ins.then_inc(s_const, 1)
            nc.gpsimd.memset(b1rows[:, :], 0.0).then_inc(s_const, 1)
            nc.gpsimd.memset(b2rows[:, :], 0.0).then_inc(s_const, 1)

            HALF = TG // 2

            def scatter(layer, g, order):
                q = lg_of(layer, g)
                for i in order:
                    k, t = divmod(i, TG)
                    if i == 0:
                        pool.wait_ge(s_route, q + 1)
                        pool.wait_ge(s_zfill, 16 * G * (layer + 2))
                    if i % HALF == 0:
                        rows = xrow[:, g * TG + t:g * TG + t + HALF, 2 * D:].bitcast(I32)
                        link(nc.gpsimd.tensor_copy(rows, ids[:, k, t:t + HALF].rearrange("p (t a) -> p t a", a=1)))
                    if q == 0 and i == 10:
                        pool.wait_ge(s_wmax, 1)
                        nc.gpsimd.partition_all_reduce(wmax[:, :], wsc[:, 0:2], P, RMAX).then_inc(s_wall, 1)
                    uses = q * (TG * TOP_K // SC_SEMS) + i // SC_SEMS
                    if uses:
                        pool.wait_ge(s_scat[i % SC_SEMS], 16 * uses)
                    pool.indirect_dma_start(
                        out=slot_x[g],
                        out_offset=bass.IndirectOffsetOnAxis(ap=slots[:, q, k, t:t + 1].bitcast(U32), axis=0),
                        in_=xrow[:, g * TG + t, :], in_offset=None).then_inc(s_scat[i % SC_SEMS], 16)

            def scatter_outputs(layer, g, i):
                n = lg_of(layer, g) * NB + i
                pool.wait_ge(s_yc, n + 1)
                for a in range(2):
                    row = rowid[:, n % YS_RING, a:a + 1].bitcast(U32)
                    pool.indirect_dma_start(
                        out=pair_y[layer][g], out_offset=bass.IndirectOffsetOnAxis(ap=row, axis=0),
                        in_=ysb[:, n % YS_RING, a, :], in_offset=None).then_inc(s_yst[a][n % YS_RING], 16)

            pool.wait_ge(s_zero, 3)
            scatter(0, 0, range(TG * TOP_K))
            for layer in range(LAYERS):
                if layer:
                    scatter(1, 0, range(TG * TOP_K))
                done_dmas = 0
                for i in range(NB):
                    upto = min(TG * TOP_K, 8 + 3 * i // 2)
                    scatter(layer, 1, range(done_dmas, upto))
                    done_dmas = upto
                    scatter_outputs(layer, 0, i)
                for i in range(NB):
                    if i < TG:
                        outputs_of_tile(pool, layer, 0, i)
                    scatter_outputs(layer, 1, i)

        @block.scalar
        def _(act):
            act.dma_start(ldt, log_dt.rearrange("(d a) -> d a", a=1)).then_inc(s_s4, 16)
            act.dma_start(sbt, s4_b).then_inc(s_s4, 16)
            act.dma_start(sct, s4_c).then_inc(s_s4, 16)
            act.dma_start(dcol, s4_d.rearrange("(d a) -> d a", a=1)).then_inc(s_s4, 16)
            act.wait_ge(s_zero, 1)
            for g in range(G):
                act.dma_start(slot_x[g].rearrange("(t p) c -> p t c", p=P)[:, :, 0:2 * D],
                              zero16.rearrange("p (a c) -> p a c", a=1).to_broadcast([P, 2 * NB, 2 * D])).then_inc(s_zfill, 16)
            act.wait_ge(s_zero, 2)
            for g in range(G):
                act.dma_start(slot_x[g].rearrange("(t p) c -> p t c", p=P)[:, :, 2 * D:], spare[:, :, :].bitcast(F16)).then_inc(s_zfill, 16)
            act.wait_ge(s_bzero, 2)
            for row in (0, 32):
                act.dma_start(b1f[row:row + E * HC, :], b1.rearrange("e (k q) -> (e k) q", k=HC)).then_inc(s_b1, 16)
            for row in (0, 32, 64):
                act.dma_start(b2f[row:row + E, :], b2).then_inc(s_b2, 16)

            LOWER, UPPER = range(TG // 2), range(TG // 2, TG)

            def normalise(kind, layer, g, tiles=None):
                def copy(m):
                    act.wait_ge(s_xnt, m + 1)
                    if m >= XNT_RING:
                        act.wait_ge(s_gate, m - XNT_RING + 1)
                    nc.scalar.activation(xnt[:, m % XNT_RING, :], TB[m % XNT_RING][:, 0:P], ACT.Copy).then_inc(s_xntc, 1)

                gate_tile = lg_of(layer, g) * TG
                tiles = HALVES[kind] if tiles is None else tiles
                for i in tiles:
                    n = norm_base(kind, layer, g) + i - HALVES[kind][0]
                    act.wait_ge(s_stat, n + 1)
                    if n >= XN_RING:
                        act.wait_ge(s_xl, n - XN_RING + 1)
                    if kind == "router" and i >= XN_RING:
                        act.wait_ge(s_xnt, gate_tile + i - XN_RING + 1)
                    nc.scalar.activation(xn[:, n % XN_RING, :], xa[:, g * TG + i, :], ACT.Identity,
                                         scale=rstd[:, i:i + 1], bias=nmr[:, i:i + 1]).then_inc(s_xn, 1)
                    if kind == "router" and i >= tiles[0] + 2:
                        copy(gate_tile + i - 2)
                if kind == "router":
                    copy(gate_tile + tiles[-1] - 1)
                    copy(gate_tile + tiles[-1])

            def router_exps(layer, g):
                q = lg_of(layer, g)
                act.wait_ge(s_rsub, 2 * q + 1)
                nc.scalar.activation(sc[:, :, :], lg[:, :, :], ACT.Exp).then_inc(s_rexp, 1)
                act.wait_ge(s_rsub, 2 * q + 2)
                nc.scalar.activation(m2[:, :], mt[:, :], ACT.Exp).then_inc(s_rexp, 1)

            def reversed_copies(g):
                for i in range(TG // 2):
                    n = g * (TG // 2) + i
                    act.wait_ge(s_rev, n + 1)
                    nc.scalar.activation(xparts[:, 2 * n:2 * n + 2, :],
                                         CBK[n % 2][:, :].rearrange("p (t r) -> p t r", t=2), ACT.Copy).then_inc(s_revc, 1)

            def w1_high():
                act.wait_ge(s_kin, 1)
                for k in range(HC):
                    nc.scalar.activation(w1part(0, k), w1chunk(k), ACT.Copy,
                                         scale=wsc[:, 2:3]).then_inc(s_wh, 1)

            def w2_high():
                for k in range(HC):
                    nc.scalar.activation(w2part(0, k), w2chunk(k), ACT.Copy,
                                         scale=wsc[:, 3:4]).then_inc(s_wh, 1)

            def kernel_power(n):
                nc.scalar.activation(kexp[:, bass.ds(n, 1), :].rearrange("p a l -> p (a l)"), kramp, ACT.Exp,
                                     scale=loga[:, bass.ds(n, 1)]).then_inc(s_kexp, 1)

            def experts(layer, g, kernel=False):
                base = lg_of(layer, g) * NB

                def copy_xt(n, v):
                    act.wait_ge(s_xt, n + 1)
                    if not first(n, 2):
                        act.wait_ge(s_h, 2 * n - 2)
                    nc.scalar.activation(xt[:, v % 2, :], XB[v % 2][:, 0:BR].bitcast(F16), ACT.Copy).then_inc(s_xtc, 1)

                def relu(n, v):
                    for j in range(2):
                        act.wait_ge(s_h, 2 * n + j + 1)
                        if not first(n, 2) and j == 0:
                            act.wait_ge(s_y, n - 1)
                        nc.scalar.activation(hh[:, v % 2, j * 512:(j + 1) * 512], HB[2 * (v % 2) + j][:, :],
                                             ACT.Relu).then_inc(s_relu, 1)

                def output(n, v):
                    act.wait_ge(s_y, n + 1)
                    if not first(n, YS_RING):
                        for a in range(2):
                            act.wait_ge(s_yst[a][v % YS_RING], (n - v % YS_RING) * (16 // YS_RING))
                    nc.scalar.activation(ysb[:, v % YS_RING, :, :],
                                         YB[v % 2][:, :].rearrange("p (a s c) -> p a s c", a=2, s=2)[:, :, 0, :],
                                         ACT.Copy).then_inc(s_ya, 1)

                copy_xt(base, base)

                def blocks(n0, r, start, end):
                    powers = kernel and not start and not end

                    def kernel_powers(u, part):
                        for i in range(STATES_PER_BLOCK // 2):
                            kernel_power(((r - 1) * ROUND + u) * STATES_PER_BLOCK + part * (STATES_PER_BLOCK // 2) + i)

                    for u, v in block_steps(base, end):
                        if not (end and (u, v) == block_steps(base, end)[-1]):
                            copy_xt(n0 + u + 1, v + 1)
                        if powers:
                            kernel_powers(u, 0)
                        relu(n0 + u, v)
                        if powers:
                            kernel_powers(u, 1)
                        if not start or u:
                            output(n0 + u - 1, v - 1)
                run_rounds(act, base, blocks)
                output(base + NB - 1, base + NB - 1)

            act.wait_ge(s_s4, 64)
            nc.scalar.activation(dtt, ldt, ACT.Exp).then_inc(s_ac, 1)
            normalise("router", 0, 0)
            act.wait_ge(s_kt, 1)
            nc.scalar.activation(th, dta, ACT.Tanh, scale=0.5).then_inc(s_ac, 1)
            router_exps(0, 0)
            normalise("router", 0, 1, LOWER)
            w1_high()
            normalise("router", 0, 1, UPPER)
            w2_high()
            router_exps(0, 1)
            act.wait_ge(s_kt, 2)
            experts(0, 0, kernel=True)
            experts(0, 1)
            reversed_copies(0)
            normalise("conv_a", 1, 1)
            normalise("conv_b", 1, 1)
            reversed_copies(1)
            normalise("router", 1, 0)
            router_exps(1, 0)
            normalise("router", 1, 1)
            router_exps(1, 1)
            experts(1, 0)
            experts(1, 1)

        @block.vector
        def _(dve):
            V = nc.vector
            done = [0]

            def link(ins):
                done[0] += 1
                ins.then_inc(s_chain, 1)
                dve.wait_ge(s_chain, done[0])

            def x_loaded(t):
                if t % (NT // 4) == 0:
                    dve.wait_ge(s_x[t // (NT // 4)], 16)

            def group_tiles(g, cols):
                return slice(g * TG + cols.start, g * TG + cols.stop)

            def newton_start(g, cols, steps=2):
                var, a, v, r = mv[:, group_tiles(g, cols), 1], nt1[:, cols], nv[:, cols], rstd[:, cols]
                V.tensor_scalar(v, var, EPS, -0.5, ALU.add, ALU.mult)
                link(V.tensor_scalar(a, var, EPS, None, ALU.add))
                link(V.tensor_scalar(r.bitcast(I32), a.bitcast(I32), -0.5, float(0x5F3759DF), ALU.mult, ALU.add))
                for _ in range(steps):
                    newton_step(cols)

            def newton_step(cols):
                a, v, r = nt1[:, cols], nv[:, cols], rstd[:, cols]
                link(V.tensor_tensor(a, r, v, ALU.mult))
                link(V.tensor_tensor(a, a, r, ALU.mult))
                link(V.scalar_tensor_tensor(r, a, 1.5, r, ALU.add, ALU.mult))

            def newton_end(g, cols):
                newton_step(cols)
                return V.scalar_tensor_tensor(nmr[:, cols], mv[:, group_tiles(g, cols), 0], -1.0, rstd[:, cols], ALU.mult, ALU.mult)

            def deviations(g, cols):
                newton_start(g, slice(cols[0], cols[-1] + 1))
                newton_end(g, slice(cols[0], cols[-1] + 1)).then_inc(s_stat, len(cols))

            def statistics(g, cols, wait_input=None):
                for i in cols:
                    if wait_input:
                        wait_input(g * TG + i)
                    ins = V.bn_stats(st6[:, i, :], xa[:, g * TG + i, :])
                link(ins)
                for i in cols:
                    ins = V.bn_aggr(mv[:, g * TG + i, :], st6[:, i, :])
                link(ins)

            def split_tiles(kind, layer, g, tiles=None):
                tiles = HALVES[kind] if tiles is None else tiles
                for i in tiles[::2]:
                    n, t = norm_base(kind, layer, g) + i - HALVES[kind][0], g * TG + i
                    x, high, low = xn[:, n % XN_RING:n % XN_RING + 2, :], xhl[:, t:t + 2, 0, :], xhl[:, t:t + 2, 1, :]
                    dve.wait_ge(s_xn, n + 2)
                    link(V.tensor_copy(high, x))
                    V.tensor_tensor(low, x, high, ALU.subtract).then_inc(s_xl, 2)

            def bc_e(a):
                return a.rearrange("p (t a) -> p t a", a=1).to_broadcast([P, TG, E])

            def bc_t(a):
                return a.rearrange("p (a e) -> p a e", a=1).to_broadcast([P, TG, E])

            def route(layer, g, beside=()):
                q = lg_of(layer, g)
                dve.wait_ge(s_gate, (q + 1) * TG)
                ins = V.tensor_tensor(lg[:, :, :], LG[:, 0:TE].rearrange("p (t e) -> p t e", e=E), bc_t(bgs[:, :]), ALU.add)
                ins.then_inc(s_logit, 1)
                dve.wait_ge(s_logit, q + 1)
                link(V.tensor_reduce(m1[:, :], lg[:, :, :], AX.X, ALU.max))
                V.tensor_tensor(lg[:, :, :], lg[:, :, :], bc_e(m1[:, :]), ALU.subtract).then_inc(s_rsub, 1)
                if beside:
                    beside[0]()
                dve.wait_ge(s_rexp, 2 * q + 1)
                link(V.tensor_reduce(m1[:, :], sc[:, :, :], AX.X, ALU.add))
                link(V.reciprocal(m2[:, :], m1[:, :]))
                link(V.tensor_tensor(sc[:, :, :], sc[:, :, :], bc_e(m2[:, :]), ALU.mult))
                for k, m in ((0, m1), (1, m2)):
                    link(V.tensor_reduce(m[:, :], sc[:, :, :], AX.X, ALU.max))
                    link(V.tensor_tensor(eq[:, :, :], sc[:, :, :], bc_e(m[:, :]), ALU.is_equal))
                    link(V.tensor_tensor(eq[:, :, :], eq[:, :, :], bc_t(prio[:, :]), ALU.mult))
                    link(V.tensor_reduce(mt[:, :], eq[:, :, :], AX.X, ALU.max))
                    link(V.tensor_tensor(ohk[k], eq[:, :, :], bc_e(mt[:, :]), ALU.is_equal))
                    if k == 0:
                        link(V.scalar_tensor_tensor(sc[:, :, :], ohk[0], -2.0, sc[:, :, :], ALU.mult, ALU.add))
                V.tensor_tensor(ohs[:, :, :], ohk[0], ohk[1], ALU.add).then_inc(s_oh, 1)
                V.tensor_tensor(mt[:, :], m2[:, :], m1[:, :], ALU.subtract).then_inc(s_rsub, 1)
                if beside:
                    beside[1]()
                before = CBK[0][:, 0:TE].rearrange("p (t e) -> p t e", e=E)
                totals = CBK[0][:, TE:2 * TE]
                dve.wait_ge(s_pre, q + 1)
                earlier = eq[:, :, :].rearrange("p t e -> p (t e)")
                flat = cum.rearrange("p e t -> p (e t)")
                link(V.tensor_tensor_scan(flat, segm[:, :, :].rearrange("p e t -> p (e t)"), totals, 0.0, ALU.mult, ALU.add))
                V.tensor_scalar(cnti[:, :], cum[:, :, TG - 1], float(BR - 1), None, ALU.add)
                link(V.tensor_tensor(earlier, flat, totals, ALU.subtract))
                link(V.tensor_scalar(cnti[:, :], cnti[:, :], -BR, None, ALU.bitwise_and))
                link(V.tensor_copy(cnt[:, :], cnti[:, :]))
                link(V.tensor_tensor_scan(ends[:, :], one8[:, :], cnt[:, :], 0.0, ALU.mult, ALU.add))
                V.tensor_tensor(cnt[:, :], ends[:, :], cnt[:, :], ALU.subtract)
                dve.wait_ge(s_xl, norm_base("router", layer, g) + TG)
                link(V.tensor_tensor(et1, ends[0:1, :].rearrange("p (a e) -> p a e", a=1).to_broadcast([1, NB, E]),
                                     tstart[:, :, :], ALU.is_le))
                V.tensor_reduce(et2[:, :], et1, AX.X, ALU.add)
                link(V.tensor_tensor(pos, earlier.rearrange("p (e t) -> p t e", e=E), bc_t(cnt[:, :]), ALU.add))
                V.tensor_scalar(etab[:, q * NB:(q + 1) * NB], et2[:, :], float(E - 1), None, ALU.min)
                link(V.tensor_tensor(pos, before, pos, ALU.add))
                link(V.tensor_tensor(chosen[:, :, :], oh[:, :, :],
                                     pos.rearrange("p t e -> p (t e)").rearrange("p (a n) -> p a n", a=1).to_broadcast([P, TOP_K, TE]), ALU.mult))
                link(V.tensor_reduce(slotf[:, :, :], chosen[:, :, :].rearrange("p k (t e) -> p k t e", e=E), AX.X, ALU.add))
                V.tensor_copy(slots[:, q, :, :], slotf[:, :, :]).then_inc(s_route, 1)
                dve.wait_ge(s_rexp, 2 * q + 2)
                link(V.tensor_scalar(m1[:, :], m2[:, :], 1.0, None, ALU.add))
                link(V.reciprocal(mt[:, :], m1[:, :]))
                link(V.tensor_scalar(prob[:, q, 0, :], mt[:, :], 0.5, None, ALU.mult))
                link(V.tensor_tensor(prob[:, q, 1, :], prob[:, q, 0, :], m2[:, :], ALU.mult))

            def weight_maxima(i):
                st, half = (w1st, w2st)[i // 2], E * HID // 2
                dve.wait_ge((s_w1, s_w2)[i // 2], 16)
                link(V.tensor_reduce(wparts[:, i:i + 1], st[:, (i % 2) * half:(i % 2 + 1) * half], AX.X, ALU.max,
                                     apply_absolute_value=True))
                if i == 3:
                    dve.wait_ge(s_b1, 32)
                    link(V.tensor_reduce(wparts[:, 4:5], b1f, AX.X, ALU.max, apply_absolute_value=True))
                    link(V.tensor_reduce(wsc[:, 0:2], wparts[:, 0:4].rearrange("p (w h) -> p w h", w=2), AX.X, ALU.max))
                    link(V.tensor_tensor(wsc[:, 0:1], wsc[:, 0:1], wparts[:, 4:5], ALU.max))
                    V.tensor_scalar(wsc[:, 0:2], wsc[:, 0:2], TINY, None, ALU.max).then_inc(s_wmax, 1)

            def bias_rows():
                dve.wait_ge(s_wall, 1)
                link(V.tensor_scalar(wsc[:, 2:4].bitcast(I32), wmax[:, 0:2].bitcast(I32), EXPONENT, EXPONENT,
                                     ALU.bitwise_and, ALU.bitwise_xor))
                link(V.tensor_scalar(wsc[:, 4:6].bitcast(I32), wmax[:, 0:2].bitcast(I32), EXPONENT, None, ALU.bitwise_and))
                link(V.tensor_scalar(wsc[:, 4:6], wsc[:, 4:6], 0.5, None, ALU.mult))
                link(V.tensor_tensor(wsc[:, 6:7], wsc[:, 4:5], wsc[:, 5:6], ALU.mult))
                V.tensor_tensor(wsc[:, 7:8], wsc[:, 2:3], wsc[:, 3:4], ALU.mult).then_inc(s_kin, 1)
                dve.wait_ge(s_kin, 1)
                link(V.tensor_scalar(b1f, b1f, wsc[:, 2:3], None, ALU.mult))
                link(V.tensor_copy(b1rows[0:64, :], b1f[0:64, :]))
                link(V.tensor_tensor(b1rows[32:64, :], b1f[32:64, :], b1rows[32:64, :], ALU.subtract))
                dve.wait_ge(s_b2, 48)
                link(V.tensor_scalar(b2f, b2f, wsc[:, 7:8], None, ALU.mult))
                for rows in (96, 64, 32):
                    if rows < 96:
                        link(V.tensor_tensor(b2f[0:rows, :], b2f[0:rows, :], b2rows[0:rows, :], ALU.subtract))
                    link(V.tensor_copy(b2rows[0:rows, :], b2f[0:rows, :]))

            def weights_low(part, chunk, scale, i, ks):
                for k in ks:
                    dve.wait_ge(s_wh, i * HC + k + 1)
                    V.scalar_tensor_tensor(part(1, k), chunk(k), scale, part(0, k),
                                           ALU.mult, ALU.subtract).then_inc(s_wready, 1)

            def kernel_rates():
                dve.wait_ge(s_const, 17)
                dve.wait_ge(s_ac, 1)
                V.tensor_scalar(dta, nar, dtt, -0.5, ALU.mult, ALU.mult).then_inc(s_kt, 1)
                dve.wait_ge(s_kt, 1)

            def kernel_arguments():
                link(V.tensor_scalar(loga, dta, LOG_FLOOR, None, ALU.max))
                link(V.reciprocal(rn, nar))
                dve.wait_ge(s_ac, 2)
                link(V.tensor_scalar(rden, th, -1.0, 1.0, ALU.mult, ALU.add))
                link(V.reciprocal(kw, rden))
                link(V.scalar_tensor_tensor(rden, th, -4.0, kw, ALU.mult, ALU.mult))
                link(V.tensor_tensor(rden, rden, rn, ALU.mult))
                link(V.tensor_tensor(rden, rden, sbt, ALU.mult))
                V.tensor_tensor(kw, rden, sct, ALU.mult).then_inc(s_kt, 1)
                V.memset(ksums, 0.0).then_inc(s_kacc, 1)
                dve.wait_ge(s_kt, 2)

            def kernel_sums(n0, part):
                half = STATES_PER_BLOCK // 2
                dve.wait_ge(s_kexp, n0 + (part + 1) * half)
                dve.wait_ge(s_kacc, n0 + 1)
                for i in range(part * half, (part + 1) * half):
                    V.scalar_tensor_tensor(ksums[:, i, :], kexp[:, bass.ds(n0 + i, 1), :].rearrange("p a l -> p (a l)"),
                                           kw[:, bass.ds(n0 + i, 1)], ksums[:, i, :], ALU.mult, ALU.add).then_inc(s_kacc, 1)

            def kernel_rows():
                dve.wait_ge(s_kacc, N_STATE + 1)
                link(V.tensor_tensor(ksums[:, 0:2, :], ksums[:, 0:2, :], ksums[:, 2:4, :], ALU.add))
                link(V.tensor_tensor(kacc, ksums[:, 0, :], ksums[:, 1, :], ALU.add))
               
                link(V.tensor_tensor(kacc[:, 0:1], kacc[:, 0:1], dcol, ALU.add))
                link(V.tensor_reduce(kmx, kacc, AX.X, ALU.max, apply_absolute_value=True))
                link(V.tensor_scalar(kmx, kmx, 1e-30, None, ALU.max))
                link(V.tensor_scalar(kal.bitcast(I32), kmx.bitcast(I32), EXPONENT, EXPONENT, ALU.bitwise_and, ALU.bitwise_xor))
                link(V.tensor_scalar(kiv.bitcast(I32), kmx.bitcast(I32), EXPONENT, None, ALU.bitwise_and))
                link(V.tensor_scalar(kiv, kiv, 0.5, None, ALU.mult))
                V.tensor_scalar(kdiag, ident[:, :], kiv, None, ALU.mult).then_inc(s_kdiag, 1)
                link(V.tensor_scalar(kpad[:, P:, 0], kacc, kal, None, ALU.mult))
                V.scalar_tensor_tensor(kpad[:, P:, 1], kacc, kal, kpad[:, P:, 0], ALU.mult, ALU.subtract).then_inc(s_kpad, 1)

            def experts(layer, g, kernel=False, beside=None):
                base = lg_of(layer, g) * NB

                def split(n, v):
                    for j in range(2):
                        half = slice(j * 512, (j + 1) * 512)
                        dve.wait_ge(s_relu, 2 * n + j + 1)
                        V.scalar_tensor_tensor(hl[:, v % 2, half], HB[2 * (v % 2) + j][:, :], 0.0, hh[:, v % 2, half],
                                               ALU.max, ALU.subtract).then_inc(s_hl, 1)

                def output(n, v):
                    dve.wait_ge(s_ya, n + 1)
                    y = YB[v % 2][:, :].rearrange("p (a s c) -> p a s c", a=2, s=2)
                    place = ysb[:, v % YS_RING, :, :]
                    V.tensor_tensor(place, y[:, :, 1, :], place, ALU.add).then_inc(s_yc, 1)

                def keep_rows(n, v):
                    if not first(n, YS_RING):
                        for a in range(2):
                            dve.wait_ge(s_yst[a][v % YS_RING], (n - v % YS_RING) * (16 // YS_RING))
                    V.tensor_copy(rowid[:, v % YS_RING, :].rearrange("p (a c) -> p a c", c=1),
                                  xs[:, v % XS_RING, :, 2 * D:].bitcast(I32)).then_inc(s_rowid, 1)

                def blocks(n0, r, start, end):
                    def sums(u, part):
                        if kernel and not start and not end:
                            kernel_sums(((r - 1) * ROUND + u) * STATES_PER_BLOCK, part)

                    for u, v in block_steps(base, end):
                        sums(u, 0)
                        split(n0 + u, v)
                        if not start or u:
                            output(n0 + u - 1, v - 1)
                        keep_rows(n0 + u, v)
                        sums(u, 1)
                        if beside:
                            beside(r * ROUND + u)
                run_rounds(dve, base, blocks, straight=beside is not None)
                output(base + NB - 1, base + NB - 1)

            def combine(layer, g, tiles):
                q = lg_of(layer, g)
                ring = output_ring(g)

                def add(t, k):
                    tile = xa[:, g * TG + t, :]
                    return V.scalar_tensor_tensor(tile, yplace[t % ring][:, k, :], prob[:, q, k, t:t + 1], tile, ALU.mult, ALU.add)

                for i in range(0, len(tiles), 2):
                    pair = tiles[i:i + 2]
                    for t in pair:
                        dve.wait_ge(s_yg[g][t % ring], ((layer * TG + t) // ring + 1) * 16)
                        add(t, 0).then_inc(s_part, 1)
                    for t in pair:
                        dve.wait_ge(s_part, q * TG + t + 1)
                        add(t, 1).then_inc(s_comb, 1)
                dve.wait_ge(s_comb, q * TG + tiles[-1] + 1)

            LOAD_TIME = 3

            def combine_beside(i):
                if LOAD_TIME <= i < LOAD_TIME + TG:
                    combine(1, 0, [i - LOAD_TIME])

            BATCH_TILES = 4
            assert LOAD_TIME + BATCH_TILES + TG <= NB

            def first_conv_input(i):
                if i == 0:
                    dve.wait_ge(s_kinv, 1)
                    V.tensor_copy(kinv[:, :], CBK[1][:, 0:D]).then_inc(s_kinvc, 1)
                if LOAD_TIME <= i < LOAD_TIME + TG:
                    combine(0, 0, [i - LOAD_TIME])
                b, step = divmod(i - LOAD_TIME - BATCH_TILES, BATCH_TILES)
                if 0 <= b < TG // BATCH_TILES:
                    cols = range(b * BATCH_TILES, (b + 1) * BATCH_TILES)
                    sl = slice(cols[0], cols[-1] + 1)
                    if step == 0:
                        statistics(0, cols)
                    if step == 1:
                        newton_start(0, sl)
                    if step >= 2:
                        if step == 2:
                            link(newton_end(0, sl))
                            if b == 0:
                                old_parts_scattered(1)
                        two = range(cols[0] + 2 * (step - 2), cols[0] + 2 * (step - 1))
                        for i, c in enumerate(two):
                            ins = V.tensor_scalar(xm[:, i, :], xa[:, c, :], rstd[:, c:c + 1], nmr[:, c:c + 1],
                                                  ALU.mult, ALU.add)
                        link(ins)
                        high, low = (xhl[:, two[0]:two[1] + 1, part, :] for part in (0, 1))
                        link(V.tensor_copy(high, xm[:, :, :]))
                        V.tensor_tensor(low, xm[:, :, :], high, ALU.subtract).then_inc(s_xm, 1)
                        dve.wait_ge(s_xm, two[1] // 2 + 1)

            def old_parts_scattered(groups):
                for k in range(SC_SEMS):
                    dve.wait_ge(s_scat[k], 16 * groups * (TG * TOP_K // SC_SEMS))

            def scale_prob(q0, q1):
                v = prob[:, q0:q1, :, :].rearrange("p q k t -> p (q k t)")
                link(V.tensor_scalar(v, v, wsc[:, 6:7], None, ALU.mult))

            def conv_output(g, order):
                for i in order:
                    cb = conv_blocks(g)[i]
                    n = g * (D // CB) + i
                    dve.wait_ge(s_cv, n + 1)
                    tmp = cvt[:, n % 2, :].rearrange("p (t c) -> p t c", c=CB)
                    scale = kinv[:, cb * CB:(cb + 1) * CB].rearrange("p (a c) -> p a c", a=1).to_broadcast([P, TG, CB])
                    V.tensor_tensor(tmp, CVB[n % 4][:, :].rearrange("p (t c) -> p t c", c=CB), scale, ALU.mult).then_inc(s_cve, 1)
                    dve.wait_ge(s_cve, n + 1)
                    dst = xa[:, g * TG:(g + 1) * TG, cb * CB:(cb + 1) * CB]
                    link(V.tensor_tensor(dst, dst, tmp, ALU.add))

            ALL, LOWER, UPPER, BLOCKS = range(TG), range(TG // 2), range(TG // 2, TG), range(D // CB)
            statistics(0, LOWER, x_loaded)
            deviations(0, LOWER)
            statistics(0, UPPER, x_loaded)
            deviations(0, UPPER)
            kernel_rates()
            statistics(1, ALL, x_loaded)
            split_tiles("router", 0, 0)
            dve.wait_ge(s_wg, 32)
            route(0, 0, beside=(kernel_arguments, lambda: weight_maxima(0)))
            deviations(1, ALL)
            weight_maxima(1)
            weight_maxima(2)
            weight_maxima(3)
            split_tiles("router", 0, 1, LOWER)
            bias_rows()
            w1_low = lambda ks: weights_low(w1part, w1chunk, wsc[:, 2:3], 0, ks)
            w2_low = lambda ks: weights_low(w2part, w2chunk, wsc[:, 3:4], 1, ks)
            w1_low(range(HC))
            split_tiles("router", 0, 1, UPPER)
            w2_low([0])
            route(0, 1, beside=(lambda: w2_low([1]), lambda: w2_low([2, 3])))
            scale_prob(0, 2)
            experts(0, 0, kernel=True)
            kernel_rows()
            experts(0, 1, beside=first_conv_input)
            old_parts_scattered(G)
            combine(0, 1, LOWER)
            statistics(1, LOWER)
            deviations(1, LOWER)
            conv_output(0, [0])
            split_tiles("conv_a", 1, 1)
            combine(0, 1, UPPER)
            statistics(1, UPPER)
            deviations(1, UPPER)
            conv_output(0, [1, 2])
            split_tiles("conv_b", 1, 1)
            conv_output(0, [3])
            statistics(0, ALL)
            deviations(0, ALL)
            split_tiles("router", 1, 0)
            route(1, 0, beside=(lambda: conv_output(1, [0]), lambda: conv_output(1, [1])))
            conv_output(1, [2, 3])
            statistics(1, ALL)
            deviations(1, ALL)
            split_tiles("router", 1, 1)
            route(1, 1)
            scale_prob(2, 4)
            experts(1, 0)
            experts(1, 1, beside=combine_beside)
            combine(1, 1, ALL)

        @block.tensor
        def _(pe):
            def mm(o, a, b, start, stop):
                return nc.tensor.matmul(o, lhsT=a, rhs=b, start=start, stop=stop)

            def logits(layer, g):
                q = lg_of(layer, g)

                def product(n):
                    t = n - q * TG
                    pe.wait_ge(s_xntc, n + 1)
                    mm(LG[:, t * E:(t + 1) * E], xnt[:, n % XNT_RING, :], wgs[:, :], True, True).then_inc(s_gate, 1)

                if q:
                    pe.wait_ge(s_route, q)
                if layer:
                    pe.wait_ge(s_revc, G * (TG // 2))
                for t in range(TG):
                    n = q * TG + t
                    m = norm_base("router", layer, g) + t
                    pe.wait_ge(s_xn, m + 1)
                    if n >= XNT_RING:
                        pe.wait_ge(s_xntc, n - XNT_RING + 1)
                    nc.tensor.transpose(TB[n % XNT_RING][:, 0:P], xn[:, m % XN_RING, :], ident[:, :]).then_inc(s_xnt, 1)
                    if t >= 2:
                        product(n - 2)
                product(q * TG + TG - 2)
                product(q * TG + TG - 1)

            def prefix_counts(layer, g):
                q = lg_of(layer, g)
                pe.wait_ge(s_oh, q + 1)
                ohf = ohs[:, :, :].rearrange("p t e -> p (t e)")
                mm(CBK[0][:, 0:TE], before16[:, :], ohf, True, True)
                mm(CBK[0][:, TE:2 * TE].rearrange("p (e t) -> p e t", e=E), ones16[:, :],
                   ohs[:, :, :].rearrange("p t e -> p e t"), True, True).then_inc(s_pre, 1)

            er = [pe.alloc_register(f"expert{i}") for i in range(4)]
            ep = pe.alloc_register("expert_before")

            def experts(layer, g, prepare_output=None):
                base = lg_of(layer, g) * NB
                pe.wait_ge(s_route, (layer + 1) * G)

                def front(n, v):
                    pe.wait_ge(s_xs[v % XS_RING], (n - v % XS_RING) * (16 // XS_RING) + 16)
                    if not first(n, 2):
                        pe.wait_ge(s_xtc, n - 1)
                    b = XB[v % 2][:, 0:BR].bitcast(F16)
                    for a in range(2):
                        for s in range(2):
                            at = s * BR + a * P
                            last = nc.tensor.transpose(b[:, at:at + P], xs[:, v % XS_RING, a, s * P:(s + 1) * P], ident16[:, :])
                    last.then_inc(s_xt, 1)

                def hidden(n, v, e):
                    pe.wait_ge(s_xtc, n + 1)
                    xh, xl = xt[:, v % 2, 0:BR], xt[:, v % 2, BR:2 * BR]
                    for j in range(2):
                        b = HB[2 * (v % 2) + j]
                        if not first(n, 2):
                            pe.wait_ge(s_hl, 2 * n + j - 3)
                        row = sel[:, bass.ds(e * HC + 2 * j, 2)].rearrange("p (k a) -> p k a", a=1).to_broadcast([P, 2, BR])
                        mm(b[:, :].rearrange("p (k r) -> p k r", k=2), b1rows[:, :], row, True, False)
                        for k in (2 * j, 2 * j + 1):
                            o = b[:, (k % 2) * BR:(k % 2 + 1) * BR]
                            wh, wl = w1p[0][k][:, bass.ds(e * P, P)], w1p[1][k][:, bass.ds(e * P, P)]
                            mm(o, wh, xh, False, False)
                            mm(o, wh, xl, False, False)
                            last = mm(o, wl, xh, False, k % 2 == 1)
                        last.then_inc(s_h, 1)

                def output(n, v, e):
                    pe.wait_ge(s_hl, 2 * n + 2)
                    if not first(n, 2):
                        pe.wait_ge(s_yc, n - 1)
                    b = YB[v % 2][:, :].rearrange("p (a s c) -> p a s c", a=2, s=2)
                    for k in range(HC):
                        both, high = w2p[k][:, bass.ds(e * 2 * D, 2 * D)], w2p[k][:, bass.ds(e * 2 * D, D)]
                        for a in range(2):
                            at = slice(k * BR + a * P, k * BR + (a + 1) * P)
                            mm(b[:, a, :, :].rearrange("p s c -> p (s c)"), hh[:, v % 2, at], both, k == 0 and a == 0, False)
                            mm(b[:, a, 0, :], hl[:, v % 2, at], high, False, False)
                    row = b2rows[:, :].rearrange("p (a c) -> p a c", a=1).to_broadcast([P, 2, D])
                    mm(b[:, :, 0, :], sel3[:, bass.ds(e, 1)].to_broadcast([P, P]), row, False, True).then_inc(s_y, 1)

                def value(reg):
                    return pe.snap(reg, min_val=0, max_val=E - 1)

                front(base, base)

                def blocks(n0, r, start, end):
                    steps = block_steps(base, end)
                    if not start:
                        pe.reg_mov(ep, er[ROUND - 1])
                    pe.load(er[0:len(steps)], etab[0:1, bass.ds(n0, len(steps))])
                    before = None if start else value(ep)
                    for u, v in steps:
                        if not (end and (u, v) == steps[-1]):
                            front(n0 + u + 1, v + 1)
                        e = value(er[u])
                        hidden(n0 + u, v, e)
                        if prepare_output and start and u == 1:
                            prepare_output()
                        if not start or u:
                            output(n0 + u - 1, v - 1, before)
                        before = e
                run_rounds(pe, base, blocks)
                output(base + NB - 1, base + NB - 1, value(er[len(block_steps(base, True)) - 1]))

            def reverse(g):
                pe.wait_ge(s_yc, G * NB)
                for i in range(TG // 2):
                    n = g * (TG // 2) + i
                    t = 2 * n
                    if g == 0:
                        pe.wait_ge(s_xm, i + 1)
                    else:
                        kind = "conv_a" if 2 * i < TG // 2 else "conv_b"
                        pe.wait_ge(s_xl, norm_base(kind, 1, g) + 2 * i - HALVES[kind][0] + 2)
                    if n >= 2:
                        pe.wait_ge(s_revc, n - 1)
                    mm(CBK[n % 2][:, :].rearrange("p (t r) -> p t r", t=2), back16[:, :], xparts[:, t:t + 2, :], True, True).then_inc(s_rev, 1)
                pe.wait_ge(s_revc, (g + 1) * (TG // 2))

            def conv(g, order):
                for i in order:
                    cb = conv_blocks(g)[i]
                    n = g * (D // CB) + i
                    if g:
                        pe.wait_ge(s_cve, n - 3)
                    b = CVB[n % 4][:, :].rearrange("p (t c) -> p t c", c=CB)
                    for c in range(CB):
                        d = cb * CB + c
                        part = d // TC
                        if d == 0 and g == 0:
                            pe.wait_ge(s_toep, 16 * (ROUNDS - 2) * ROUND)
                        if d == D - TC and g == 0:
                            pe.wait_ge(s_tlast, 16)
                        if d == 0 and g:
                            pe.wait_ge(s_tagain, 16)
                        at = toeplitz_place(part, g) * TC + d % TC
                        th0, tl0 = toep[:, at, 0:2 * P:2], toep[:, at, 1:2 * P:2]
                        th1, tl1 = toep[:, at, 2 * P::2], toep[:, at, 2 * P + 1::2]
                        a, z = g * TG, (g + 1) * TG
                        xh, xl = xhl[:, a:z, 0, d], xhl[:, a:z, 1, d]
                        xh0, xl0 = xhl[:, a:z:2, 0, d], xhl[:, a:z:2, 1, d]
                        o, o1 = b[:, :, c], b[:, 1::2, c]
                        mm(o, th0, xh, True, False)
                        mm(o, th0, xl, False, False)
                        mm(o1, th1, xh0, False, False)
                        mm(o1, th1, xl0, False, False)
                        mm(o1, tl1, xh0, False, False)
                        last = mm(o, tl0, xh, False, True)
                    last.then_inc(s_cv, 1)

            pe.wait_ge(s_const, 17)
            pe.wait_ge(s_wg, 32)
            for g in range(G):
                logits(0, g)
                prefix_counts(0, g)
            pe.wait_ge(s_wready, 2 * HC)

            experts(0, 0)

            def kernel_scales():
                pe.wait_ge(s_kdiag, 1)
                pe.wait_ge(s_yc, NB)
                mm(CBK[1][:, 0:D], onesf, kdiag, True, True).then_inc(s_kinv, 1)
                pe.wait_ge(s_kinvc, 1)

            experts(0, 1, kernel_scales)
            reverse(0)
            conv(0, range(D // CB))
            reverse(1)
            conv(1, [0])
            logits(1, 0)
            conv(1, [1, 2])
            prefix_counts(1, 0)
            conv(1, [3])
            logits(1, 1)
            prefix_counts(1, 1)
            experts(1, 0)
            experts(1, 1)


_INS = ['L0_attn_x', 'L0_attn_log_dt', 'L0_attn_B', 'L0_attn_C', 'L0_attn_D', 'L0_ffn_W1', 'L0_ffn_b1',
        'L0_ffn_W2', 'L0_ffn_b2', 'L0_ffn_Wg', 'L0_ffn_bg']


def kernel(**inputs):
    import numpy as _np
    import concourse.bacc as _bacc
    from concourse import mybir as _mybir
    from concourse.bass_utils import run_bass_kernel_spmd as _run

    nc = _bacc.Bacc("TRN2", target_bir_lowering=False, num_devices=1)
    arrays, args = {}, []
    for name in _INS:
        a = _np.ascontiguousarray(inputs[name])
        arrays[f"in_{name}_dram"] = a
        args.append(nc.dram_tensor(f"in_{name}_dram", a.shape, _mybir.dt.from_np(a.dtype), kind="ExternalInput").ap())
    args.append(nc.dram_tensor("out_0_dram", (BATCH, LENGTH, D), _mybir.dt.float32, kind="ExternalOutput").ap())
    macaron_kernel(nc, *args)
    r = _run(nc, [arrays], core_ids=[0])
    return r.results[0]["out_0_dram"]
```
